# Optimizing a Trainium2 kernel written in Bass

```python
import numpy as np
import jax
import jax.numpy as jnp

def _softmax(x, axis=-1):
    return jax.nn.softmax(x, axis=axis)

def _gelu(x):
    return jax.nn.gelu(x, approximate=True)

def _silu(x):
    return jax.nn.silu(x)

def _sigmoid(x):
    return jax.nn.sigmoid(x)

def _layernorm(x, axis=-1, eps=1e-05):
    m = jnp.mean(x, axis=axis, keepdims=True)
    v = jnp.var(x, axis=axis, keepdims=True)
    return (x - m) / jnp.sqrt(v + eps)

def _scatter_add(tgt, idx, src, axis=0):
    return tgt.at[idx].add(src)

def _segment_sum(src, seg, n):
    return jax.ops.segment_sum(src, seg, n)
kernel_name = 'mk_gnn_preln_d1_gnn_r32_fc3a4d'

def setup_inputs(seed: int=0):
    np.random.seed(seed)
    _w = jnp.asarray

    def _rec_inputs():
        import jax
        import jax.numpy as jnp
        _gk = jax.random.key(seed)
        x = -0.0003713 + 1 * jax.random.normal(jax.random.fold_in(_gk, 1), (50000, 256), jnp.float32)
        src = jax.random.randint(jax.random.fold_in(_gk, 2), (25000,), 0, 50000, jnp.int32)
        dst = jax.random.randint(jax.random.fold_in(_gk, 3), (25000,), 0, 50000, jnp.int32)
        _o = jnp.argsort(dst, stable=True)
        src = src[_o]
        dst = dst[_o]
        edge_attr_64 = 0.000189758 + 1.00013 * jax.random.normal(jax.random.fold_in(_gk, 11), (25000, 64), jnp.float32)
        return (x, src, dst, edge_attr_64)
    x, src, dst, edge_attr_64 = _rec_inputs()

    def _L0_gnn_setup():
        import jax, jax.numpy as jnp
        import numpy as np
        N_NODES = 50000
        N_EDGES = 25000
        NODE_DIM = 256
        EDGE_DIM = 64
        HIDDEN = 512
        OUT_DIM = 256
        key = jax.random.key(seed)
        ks = jax.random.split(key, 6)
        node_features = jax.random.normal(ks[0], (N_NODES, NODE_DIM), dtype=jnp.float32)
        edge_index = jax.random.randint(ks[1], (2, N_EDGES), 0, N_NODES, dtype=jnp.int64)
        edge_features = jax.random.normal(ks[2], (N_EDGES, EDGE_DIM), dtype=jnp.float32)
        in_dim = EDGE_DIM + NODE_DIM
        W1 = jax.random.normal(ks[3], (in_dim, HIDDEN), dtype=jnp.float32) * (1.0 / np.sqrt(in_dim))
        b1 = jnp.zeros((HIDDEN,), dtype=jnp.float32)
        W2 = jax.random.normal(ks[4], (HIDDEN, OUT_DIM), dtype=jnp.float32) * (1.0 / np.sqrt(HIDDEN))
        b2 = jnp.zeros((OUT_DIM,), dtype=jnp.float32)
        return {'node_features': node_features, 'edge_index': edge_index, 'edge_features': edge_features, 'W1': W1, 'b1': b1, 'W2': W2, 'b2': b2}
    _L0_gnn_all = _L0_gnn_setup()
    _L0_gnn_in = {k: v for k, v in _L0_gnn_all.items() if k in ('W1', 'b1', 'W2', 'b2')}
    del _L0_gnn_all
    return {'x': x, 'src': src, 'dst': dst, 'edge_attr_64': edge_attr_64, 'L0_gnn_W1': _L0_gnn_in['W1'], 'L0_gnn_b1': _L0_gnn_in['b1'], 'L0_gnn_W2': _L0_gnn_in['W2'], 'L0_gnn_b2': _L0_gnn_in['b2']}

def reference(x, src, dst, edge_attr_64, L0_gnn_W1, L0_gnn_b1, L0_gnn_W2, L0_gnn_b2):
    import jax
    import jax.numpy as jnp

    def _L0_gnn_ref(node_features, edge_index, edge_features, W1, b1, W2, b2):
        import jax, jax.numpy as jnp
        import numpy as np
        N_NODES = 50000
        N_EDGES = 25000
        NODE_DIM = 256
        EDGE_DIM = 64
        HIDDEN = 512
        OUT_DIM = 256
        tgt = edge_index[1]
        agg = jax.ops.segment_sum(edge_features, tgt, num_segments=N_NODES)
        counts = jax.ops.segment_sum(jnp.ones((edge_features.shape[0],), edge_features.dtype), tgt, num_segments=N_NODES)
        agg = agg / jnp.maximum(counts, 1.0)[:, None]
        combined = jnp.concatenate([agg, node_features], axis=1)
        h = jax.nn.relu(combined @ W1 + b1)
        out = h @ W2 + b2
        return out
    edge_index = jnp.stack([src, dst])
    h = jnp.maximum(_layernorm(x, axis=-1), 0.0)
    x = x + _L0_gnn_ref(h, edge_index, edge_attr_64, L0_gnn_W1, L0_gnn_b1, L0_gnn_W2, L0_gnn_b2)
    return x

_drawn_inputs = setup_inputs


def setup_inputs(seed=0):
    import zlib

    import numpy as np

    out = dict(_drawn_inputs(seed))
    spreads = {'L0_gnn_b1': (0.0, 0.1), 'L0_gnn_b2': (0.0, 0.1)}
    factors = {}
    for name, (base, spread) in spreads.items():
        noise = np.random.default_rng([zlib.crc32(name.encode()), seed]).standard_normal(out[name].shape)
        drawn = base * np.exp(spread * noise) if base else spread * noise
        out[name] = jnp.asarray(drawn.astype(out[name].dtype))
    for name, factor in factors.items():
        out[name] = (out[name] * factor).astype(out[name].dtype)
    return out
```

```python
from contextlib import ExitStack

import concourse.bass as bass
from concourse import mybir

ALU = mybir.AluOpType
ACT = mybir.ActivationFunctionType
AX_X = mybir.AxisListType.X
F32 = mybir.dt.float32
F32R = mybir.dt.float32r
BF16 = mybir.dt.bfloat16
I32 = mybir.dt.int32
U32 = mybir.dt.uint32

P = 128
SUB = 4
TILE = SUB * P
EPS = 1e-5


def past(eng, sem, value):
    if not isinstance(value, int) or value > 0:
        eng.wait_ge(sem, value)


def build(nc, x, src, dst, edge_attr, w1, b1, w2, b2, out):
    N, D = x.shape
    E, DE = edge_attr.shape
    H = w1.shape[1]
    CD, CH = D // P, H // P
    assert w1.shape[0] == DE + D and w2.shape == (H, D) and 2 * DE == P and CD == 2 and CH == 4

    TILES = -(-N // TILE)
    LAST = N - TILE
    NEW = (TILES - 1) * TILE - LAST
    assert TILES % 2 == 0 and N % TILE

    EP, GR = 125, 10
    ER_ = E // EP
    GP = ER_ // GR
    assert EP * GP * GR == E
    KS = SUB + 1
    CAP = E - P

    SLOTS = E // EP
    NQ = 16
    BLOCKS = N // (EP * NQ)
    assert BLOCKS * EP * NQ == N

    with ExitStack() as ctx:
        def sb(name, shape, dt=F32):
            return ctx.enter_context(nc.sbuf_tensor(name, shape, dt))

        def ps(name, shape, dt=F32):
            return ctx.enter_context(nc.psum_tensor(name, shape, dt))

        def sem(name):
            return ctx.enter_context(nc.semaphore(name))

        ident = sb("ident", [P, P])
        iota_row = sb("iota_row", [P, P])
        part_id = sb("part_id", [P, 1])
        base = sb("base", [P, TILES, SUB])
        half = sb("half", [P, SUB])
        eps = sb("eps", [P, SUB])
        ones_bf = sb("ones_bf", [P, 1], BF16)
        ones_f = sb("ones_f", [P, 1])
        b2_row = sb("b2_row", [P, D])
        w1_raw = sb("w1_raw", [P, CD, H])
        wa_raw = sb("wa_raw", [P, H])
        b1_raw = sb("b1_raw", [P, H])
        w2_raw = sb("w2_raw", [P, CH, D])
        w1_hi = sb("w1_hi", [P, CD, H], F32R)
        w1_lo = sb("w1_lo", [P, CD, H], F32R)
        wa_hi = sb("wa_hi", [P, H], F32R)
        wb_lo = sb("wb_lo", [P, H], F32R)
        b1_hi = sb("b1_hi", [P, H], F32R)
        w2_hi = sb("w2_hi", [P, CH, D], F32R)
        w2_lo = sb("w2_lo", [P, CH, D], F32R)

        dst_a = sb("dst_a", [EP, ER_], I32)
        dst_b = sb("dst_b", [EP, ER_], I32)
        lasts = sb("lasts", [EP, GP])
        thresholds = sb("thresholds", [EP, KS, TILES])
        below = sb("below", [EP, GP, KS * TILES], BF16)
        falls = sb("falls", [EP, ER_])
        fall = sb("fall", [EP, 1])
        start_f = sb("start_f", [1, KS * TILES])
        start_i = sb("start_i", [1, KS * TILES], I32)
        end_f = sb("end_f", [1, SUB * TILES])
        reach = sb("reach", [1, SUB * TILES])
        longest = sb("longest", [1, 1])
        misfit = sb("misfit", [1, 1])
        flag_f = sb("flag_f", [1, 1])
        flag_i = sb("flag_i", [1, 1], I32)

        X = [sb(f"X{b}", [P, SUB, D]) for b in range(2)]
        XB = [sb(f"XB{b}", [P, SUB, D]) for b in range(2)]
        O = [sb(f"O{b}", [P, SUB, D]) for b in range(2)]
        HN = [sb(f"HN{b}", [P, SUB, D]) for b in range(2)]
        stats = [sb(f"stats{b}", [P, SUB, 6]) for b in range(2)]
        mv = [sb(f"mv{b}", [P, SUB, 2]) for b in range(2)]
        veps = [sb(f"veps{b}", [P, SUB]) for b in range(2)]
        negm = [sb(f"negm{b}", [P, SUB]) for b in range(2)]
        rstd = [sb(f"rstd{b}", [P, SUB]) for b in range(2)]
        shift = [sb(f"shift{b}", [P, SUB]) for b in range(2)]
        ER = [sb(f"ER{b}", [P, SUB, DE]) for b in range(2)]
        DW = [sb(f"DW{b}", [P, SUB], I32) for b in range(2)]
        rel = [sb(f"rel{b}", [P, SUB]) for b in range(2)]
        ES = [sb(f"ES{b}", [P, SUB, 2 * DE + 2], F32R) for b in range(2)]
        OH = [sb(f"OH{b}", [P, SUB, P], F32R) for b in range(2)]
        cnt = sb("cnt", [P, SUB])
        rcp = sb("rcp", [P, SUB])
        SS = sb("SS", [P, SUB, 2 * DE + 2])
        sums = sb("sums", [P, SUB, DE])
        AG = sb("AG", [P, SUB, 2, DE])
        HT_hi = sb("HT_hi", [P, CD, TILE], F32R)
        HT_lo = sb("HT_lo", [P, CD, TILE], F32R)
        QA = sb("QA", [P, TILE], F32R)
        QB = sb("QB", [P, TILE], F32R)
        H1_hi = sb("H1_hi", [P, CH, TILE], F32R)
        H1_lo = sb("H1_lo", [P, CH, TILE], F32R)

        g_dst = sb("g_dst", [EP, 1], I32)
        g_dstf = sb("g_dstf", [EP, 1])
        g_row = sb("g_row", [EP, EP])
        g_same = sb("g_same", [EP, EP])
        g_earlier = sb("g_earlier", [EP, EP])
        g_count = sb("g_count", [EP, 1])
        g_move = sb("g_move", [EP, 1])
        g_idx = sb("g_idx", [EP, 1], I32)
        g_edges = sb("g_edges", [EP, DE + 1])
        g_old = sb("g_old", [EP, DE + 1])
        g_new = sb("g_new", [EP, DE + 1])
        g_blk = sb("g_blk", [EP, NQ, DE + 1])
        g_cnt = sb("g_cnt", [EP, NQ, 1])
        g_rcp = sb("g_rcp", [EP, NQ, 1])
        g_mean = sb("g_mean", [EP, NQ, DE])
        g_ids = sb("g_ids", [EP, N // EP], I32)
        g_sums_dram = nc.dram_tensor("g_sums_dram", (N + EP, DE + 1), F32).ap()
        g_means_dram = nc.dram_tensor("g_means_dram", (N, DE), F32).ap()
        g_ids_dram = nc.dram_tensor("g_ids_dram", (N, 1), I32).ap()

        PH = [ps(f"PH{c}", [P, TILE]) for c in range(CD)]
        PA = ps("PA", [P, TILE])
        PS = ps("PS", [P, 2, 256])
        P1 = [ps(f"P1{i}", [P, TILE]) for i in range(2)]
        P2 = [ps(f"P2{i}", [P, 2, D]) for i in range(2)]

        s_const = sem("s_const")
        s_w = [sem(f"s_w{i}") for i in range(4)]
        s_zero = sem("s_zero")
        s_dst = sem("s_dst")
        s_whi = sem("s_whi")
        s_wlo = sem("s_wlo")
        s_below = sem("s_below")
        s_fall = sem("s_fall")
        s_found = sem("s_found")
        s_srch = sem("s_srch")
        s_start = sem("s_start")
        s_x = [sem(f"s_x{b}") for b in range(2)]
        s_win = [sem(f"s_win{b}") for b in range(2)]
        s_xb = sem("s_xb")
        s_stats = sem("s_stats")
        s_mv = sem("s_mv")
        s_pool = sem("s_pool")
        s_norm = sem("s_norm")
        s_ln = sem("s_ln")
        s_rel = sem("s_rel")
        s_ehi = sem("s_ehi")
        s_elo = sem("s_elo")
        s_oh = sem("s_oh")
        s_sum = sem("s_sum")
        s_sc = sem("s_sc")
        s_cnt = sem("s_cnt")
        s_rcp = sem("s_rcp")
        s_hl = sem("s_hl")
        s_agg = sem("s_agg")
        s_th = sem("s_th")
        s_ta = sem("s_ta")
        s_hhi = sem("s_hhi")
        s_hlo = sem("s_hlo")
        s_qhi = sem("s_qhi")
        s_qlo = sem("s_qlo")
        s_l1 = sem("s_l1")
        s_1hi = sem("s_1hi")
        s_1lo = sem("s_1lo")
        s_l2 = sem("s_l2")
        s_fin = sem("s_fin")
        s_out = [sem(f"s_out{b}") for b in range(2)]
        s_gz = sem("s_gz")
        s_gstep = sem("s_gstep")
        s_gclear = sem("s_gclear")
        s_gnum = sem("s_gnum")
        s_gin = sem("s_gin")
        s_gold = sem("s_gold")
        s_gv = sem("s_gv")
        s_gp = sem("s_gp")
        s_gput = sem("s_gput")
        s_gn = sem("s_gn")
        s_gnv = sem("s_gnv")
        s_gout = sem("s_gout")
        s_gid = sem("s_gid")
        s_gst = sem("s_gst")

        block = ctx.enter_context(nc.Block())

        @block.sync
        def _(sp):
            sp.wait_ge(s_zero, 1)
            sp.dma_start(dst_a[:], dst.rearrange("(p r) -> p r", p=EP)).then_inc(s_dst, 16)
            sp.dma_start(dst_b[0:EP - 1, :],
                         dst[1:1 + (EP - 1) * ER_].rearrange("(p r) -> p r", r=ER_)).then_inc(s_dst, 16)
            sp.dma_start(dst_b[EP - 1:EP, 0:ER_ - 1],
                         dst[1 + (EP - 1) * ER_:E].rearrange("(p r) -> p r", p=1)).then_inc(s_dst, 16)

            def load_x(t, b):
                past(sp, s_ln, SUB * (t - 1))
                past(sp, s_xb, t - 1)
                past(sp, s_elo, t - 1)
                past(sp, s_rel, t - 1)
                first = LAST if isinstance(t, int) and t == TILES - 1 else t * TILE
                rows = x[first:first + TILE, :] if isinstance(t, int) else x[bass.ds(first, TILE), :]
                sp.dma_start(X[b][:], rows.rearrange("(j p) d -> p j d", p=P)).then_inc(s_x[b], 16)

            flag = []

            def load_windows(t, b):
                where = [start_i[0:1, t + k * TILES:t + k * TILES + 1] if isinstance(t, int)
                         else start_i[0:1, bass.ds(t + k * TILES, 1)] for k in range(SUB)]
                with sp.If(flag[0] == 0):
                    for k in range(SUB):
                        s = sp.value_load(where[k], min_val=0, max_val=CAP)
                        sp.dma_start(ER[b][:, k, :], edge_attr[bass.ds(s, P), :]).then_inc(s_win[b], 16)
                        sp.dma_start(DW[b][:, k:k + 1],
                                     dst[bass.ds(s, P)].rearrange("(p o) -> p o", o=1)).then_inc(s_win[b], 16)
                with sp.Else():
                    for k in range(SUB):
                        s = sp.value_load(where[k], min_val=0, max_val=N - P)
                        sp.dma_start(ER[b][:, k, :], g_means_dram[bass.ds(s, P), :]).then_inc(s_win[b], 16)
                        sp.dma_start(DW[b][:, k:k + 1], g_ids_dram[bass.ds(s, P), :]).then_inc(s_win[b], 16)

            def store(t, b):
                sp.wait_ge(s_fin, 2 * t + 2)
                if isinstance(t, int) and t == TILES - 1:
                    j, p = NEW // P, NEW % P
                    rows = out[N - TILE + NEW:N - TILE + (j + 1) * P, :]
                    sp.dma_start(rows, O[b][p:P, j, :]).then_inc(s_out[b], 16)
                    sp.dma_start(out[N - TILE + (j + 1) * P:N, :].rearrange("(j p) d -> p j d", p=P),
                                 O[b][:, j + 1:SUB, :]).then_inc(s_out[b], 16)
                else:
                    rows = out[t * TILE:(t + 1) * TILE, :] if isinstance(t, int) else out[bass.ds(t * TILE, TILE), :]
                    sp.dma_start(rows.rearrange("(j p) d -> p j d", p=P), O[b][:]).then_inc(s_out[b], 16)

            load_x(0, 0)
            load_x(1, 1)
            sp.wait_ge(s_start, 1)
            flag.append(sp.value_load(flag_i[0:1, 0:1], min_val=0, max_val=1 << 20))
            with sp.If(flag[0] != 0):
                sp.wait_ge(s_gout, 16 * BLOCKS)
                sp.wait_ge(s_gid, 16)
                sp.wait_ge(s_gst, 1)
            load_windows(0, 0)
            load_windows(1, 1)
            load_x(2, 0)
            load_windows(2, 0)
            for t in range(2):
                load_x(t + 3, (t + 3) % 2)
                load_windows(t + 3, (t + 3) % 2)
                store(t, t % 2)
            with sp.Fori(1, TILES // 2 - 2) as i:
                for h in range(2):
                    load_x(2 * i + (h + 3), (h + 3) % 2)
                    load_windows(2 * i + (h + 3), (h + 3) % 2)
                    store(2 * i + h, h)
            for t in range(TILES - 4, TILES):
                if t + 3 < TILES:
                    load_x(t + 3, (t + 3) % 2)
                    load_windows(t + 3, (t + 3) % 2)
                store(t, t % 2)
            sp.wait_ge(s_out[0], 16 * (TILES // 2))
            sp.wait_ge(s_out[1], 16 * (TILES // 2 + 1))

        @block.gpsimd
        def _(pool):
            pool.memset(dst_b[:], 1 << 20).then_inc(s_zero, 1)
            pool.memset(b1_raw[:], 0.0).then_inc(s_zero, 1)
            pool.iota(thresholds[:], pattern=[[P, KS], [TILE, TILES]], base=0, channel_multiplier=0,
                      allow_small_or_imprecise_dtypes=True).then_inc(s_zero, 1)
            pool.wait_ge(s_zero, 3)
            pool.iota(thresholds[:, :, TILES - 1:TILES], pattern=[[P, KS], [0, 1]], base=LAST, channel_multiplier=0,
                      allow_small_or_imprecise_dtypes=True).then_inc(s_const, 1)
            pool.memset(ones_bf[:], 1.0).then_inc(s_const, 1)
            pool.memset(ones_f[:], 1.0).then_inc(s_const, 1)
            pool.iota(iota_row[:], pattern=[[1, P]], base=0, channel_multiplier=0,
                      allow_small_or_imprecise_dtypes=True).then_inc(s_const, 1)
            pool.iota(part_id[:], pattern=[[0, 1]], base=0, channel_multiplier=1,
                      allow_small_or_imprecise_dtypes=True).then_inc(s_const, 1)
            pool.memset(half[:], -0.5).then_inc(s_const, 1)
            pool.memset(eps[:], EPS).then_inc(s_const, 1)
            pool.iota(base[:], pattern=[[TILE, TILES], [P, SUB]], base=0, channel_multiplier=0,
                      allow_small_or_imprecise_dtypes=True).then_inc(s_const, 1)
            pool.wait_ge(s_const, 8)
            pool.iota(base[:, TILES - 1, :], pattern=[[P, SUB]], base=LAST, channel_multiplier=0,
                      allow_small_or_imprecise_dtypes=True).then_inc(s_const, 1)
            for b in range(2):
                pool.memset(ES[b][:, :, 2 * DE:].bitcast(F32), 1.0).then_inc(s_const, 1)
            pool.wait_ge(s_const, 11)
            pool.memset(QB[DE:P, :].bitcast(F32), 1.0).then_inc(s_const, 1)
            pool.wait_ge(s_const, 12)
            pool.memset(ident[:], 0.0).then_inc(s_const, 1)
            pool.wait_ge(s_const, 13)
            pool.affine_select(out=ident[:], in_=ident[:], compare_op=ALU.not_equal, fill=1.0, base=0,
                               pattern=[[-1, P]], channel_multiplier=1).then_inc(s_const, 1)

            def norm(t, b):
                pool.wait_ge(s_mv, SUB * t + SUB)
                past(pool, s_ln, SUB * (t - 1))
                pool.tensor_tensor(veps[b][:], mv[b][:, :, 1], eps[:], ALU.add).then_inc(s_pool, 1)
                pool.tensor_scalar(negm[b][:], mv[b][:, :, 0], -1.0, None, ALU.mult).then_inc(s_pool, 1)
                pool.wait_ge(s_pool, 3 * t + 2)
                pool.tensor_tensor(rstd[b][:], veps[b][:], half[:], ALU.pow).then_inc(s_pool, 1)
                pool.wait_ge(s_pool, 3 * t + 3)
                pool.tensor_tensor(shift[b][:], negm[b][:], rstd[b][:], ALU.mult).then_inc(s_norm, 1)

            def edges(t, b):
                pool.wait_ge(s_ehi, t + 1)
                pool.tensor_tensor(ES[b][:, :, DE:2 * DE], ER[b][:], ES[b][:, :, 0:DE],
                                   ALU.subtract).then_inc(s_elo, 1)

            def residual_in(t, b):
                past(pool, s_fin, 2 * (t - 1))
                pool.wait_ge(s_x[b], 16 * (t // 2 + 1) if isinstance(t, int) else 8 * t + (16 - 8 * b))
                pool.tensor_tensor(XB[b][:], X[b][:], b2_row[:].unsqueeze(1).to_broadcast([P, SUB, D]),
                                   ALU.add).then_inc(s_xb, 1)

            def means(t):
                pool.wait_ge(s_sc, 2 * t + 2)
                pool.tensor_tensor(sums[:], SS[:, :, 0:DE], SS[:, :, DE:2 * DE], ALU.add).then_inc(s_hl, 1)
                pool.wait_ge(s_hl, t + 1)
                pool.wait_ge(s_rcp, t + 1)
                past(pool, s_ta, t)
                pool.tensor_tensor(AG[:], sums[:].unsqueeze(2).to_broadcast([P, SUB, 2, DE]),
                                   rcp[:].unsqueeze(2).unsqueeze(3).to_broadcast([P, SUB, 2, DE]),
                                   ALU.mult).then_inc(s_agg, 1)

            pool.wait_ge(s_w[3], 48)
            pool.wait_ge(s_start, 1)
            flag = pool.value_load(flag_i[0:1, 0:1], min_val=0, max_val=1 << 20)
            with pool.If(flag != 0):
                zero = below[:, 0:GP // 2, :].rearrange("p a b -> p (a b)").bitcast(F32)
                width = zero.shape[1]
                pool.wait_ge(s_found, 1)
                pool.memset(zero, 0.0).then_inc(s_gz, 1)
                pool.wait_ge(s_gz, 1)
                flat = g_sums_dram.rearrange("n d -> (n d)")
                total = (N + EP) * (DE + 1)
                per = total // EP
                assert per * EP == total
                rows = flat.rearrange("(p r) -> p r", p=EP)
                pieces = [(a, min(a + width, per)) for a in range(0, per, width)]
                for a, z in pieces:
                    pool.dma_start(rows[:, a:z], zero[:, 0:z - a]).then_inc(s_gclear, 16)
                pool.iota(g_ids[:], pattern=[[1, N // EP]], base=0, channel_multiplier=N // EP).then_inc(s_gnum, 1)
                pool.wait_ge(s_gnum, 1)
                pool.dma_start(g_ids_dram.rearrange("(p r) o -> p (r o)", p=EP), g_ids[:]).then_inc(s_gid, 16)
                pool.memset(g_edges[:, DE:DE + 1], 1.0).then_inc(s_gz, 1)
                pool.wait_ge(s_gz, 2)
                pool.wait_ge(s_gclear, 16 * len(pieces))
                with pool.Fori(0, SLOTS) as i:
                    pool.dma_start(g_edges[:, 0:DE], edge_attr[bass.ds(i * EP, EP), :]).then_inc(s_gin, 16)
                    pool.dma_start(g_dst[:], dst[bass.ds(i * EP, EP)].rearrange("(p o) -> p o", o=1)).then_inc(s_gin, 16)
                    pool.wait_ge(s_gin, 32 * i + 32)
                    pool.sem_inc(s_gstep, 1)
                    pool.indirect_dma_start(g_old[:], None, g_sums_dram[:, :],
                                            bass.IndirectOffsetOnAxis(ap=g_dst[:].bitcast(U32), axis=0)).then_inc(s_gold, 16)
                    pool.wait_ge(s_gv, 9 * i + 9)
                    pool.sem_inc(s_gstep, 1)
                    pool.indirect_dma_start(g_sums_dram[:, :],
                                            bass.IndirectOffsetOnAxis(ap=g_idx[:].bitcast(U32), axis=0),
                                            g_new[:], None).then_inc(s_gput, 16)
                    pool.wait_ge(s_gput, 16 * i + 16)
                with pool.Fori(0, BLOCKS) as i:
                    pool.dma_start(g_blk[:], g_sums_dram[bass.ds(i * (EP * NQ), EP * NQ), :]
                                   .rearrange("(p q) d -> p q d", p=EP)).then_inc(s_gn, 16)
                    pool.wait_ge(s_gnv, 3 * i + 3)
                    pool.dma_start(g_means_dram[bass.ds(i * (EP * NQ), EP * NQ), :]
                                   .rearrange("(p q) d -> p q d", p=EP), g_mean[:]).then_inc(s_gout, 16)
                    pool.wait_ge(s_gout, 16 * i + 16)
            norm(0, 0)
            edges(0, 0)
            residual_in(0, 0)
            means(0)
            norm(1, 1)
            edges(1, 1)
            residual_in(1, 1)
            for t in range(2):
                means(t + 1)
                norm(t + 2, t % 2)
                edges(t + 2, t % 2)
                residual_in(t + 2, t % 2)
            with pool.Fori(1, TILES // 2 - 1) as i:
                for h in range(2):
                    means(2 * i + (h + 1))
                    norm(2 * i + (h + 2), h)
                    edges(2 * i + (h + 2), h)
                    residual_in(2 * i + (h + 2), h)
            means(TILES - 1)

        @block.scalar
        def _(act):
            act.dma_start(b2_row[:], b2.rearrange("(o d) -> o d", o=1).to_broadcast([P, D])).then_inc(s_w[3], 16)
            act.dma_start(w1_raw[:], w1[DE:DE + D, :].rearrange("(c p) h -> p c h", p=P)).then_inc(s_w[0], 16)
            for a in range(2):
                act.dma_start(wa_raw[a * DE:(a + 1) * DE, :], w1[0:DE, :]).then_inc(s_w[1], 16)
            act.wait_ge(s_zero, 3)
            for p in (64, 96):
                act.dma_start(b1_raw[p:p + 1, :], b1.rearrange("(o h) -> o h", o=1)).then_inc(s_w[2], 16)
            for a in range(2):
                act.dma_start(w2_raw[:, 2 * a:2 * a + 2, :],
                              w2[2 * a * P:2 * (a + 1) * P, :].rearrange("(c p) d -> p c d", p=P)).then_inc(s_w[3], 16)

            def layernorm(t, b):
                past(act, s_th, 2 * (t - 1))
                act.wait_ge(s_norm, t + 1)
                for j in range(SUB):
                    act.activation(HN[b][:, j, :], X[b][:, j, :], ACT.Relu, bias=shift[b][:, j:j + 1],
                                   scale=rstd[b][:, j:j + 1]).then_inc(s_ln, 1)

            def edges_high(t, b):
                act.wait_ge(s_win[b], 128 * (t // 2 + 1) if isinstance(t, int) else 64 * t + (128 - 64 * b))
                past(act, s_sum, 2 * (t - 1))
                act.activation(ES[b][:, :, 0:DE], ER[b][:], ACT.Copy).then_inc(s_ehi, 1)

            def transposed_high(t):
                past(act, s_l1, CH * t)
                for c in range(CD):
                    act.wait_ge(s_th, 2 * t + c + 1)
                    act.activation(HT_hi[:, c, :], PH[c][:], ACT.Copy).then_inc(s_hhi, 1)
                act.wait_ge(s_ta, t + 1)
                act.activation(QA[:], PA[:], ACT.Copy).then_inc(s_qhi, 1)
                act.activation(QB[0:DE, :], PA[0:DE, :], ACT.Copy).then_inc(s_qhi, 1)

            def sums_out(t, q):
                act.wait_ge(s_sum, 2 * t + q + 1)
                past(act, s_agg, t)
                act.activation(SS[:, 2 * q:2 * q + 2, :], PS[:, :, 0:2 * DE + 2], ACT.Copy).then_inc(s_sc, 1)

            def hidden_high(t, later=True):
                for m in range(CH):
                    act.wait_ge(s_l1, CH * t + m + 1)
                    if m == 0:
                        past(act, s_l2, 2 * t)
                    act.activation(H1_hi[:, m, :], P1[m % 2][:], ACT.Relu).then_inc(s_1hi, 1)
                    if m < 2 and later:
                        sums_out(t + 1, m)

            act.wait_ge(s_w[0], 16)
            act.activation(w1_hi[:], w1_raw[:], ACT.Copy).then_inc(s_whi, 1)
            act.wait_ge(s_w[1], 32)
            act.activation(wa_hi[:], wa_raw[:], ACT.Copy).then_inc(s_whi, 1)
            act.wait_ge(s_w[2], 32)
            act.activation(b1_hi[DE:P, :], b1_raw[DE:P, :], ACT.Copy).then_inc(s_whi, 1)
            act.activation(wb_lo[64:96, :], b1_raw[64:96, :], ACT.Copy).then_inc(s_whi, 1)
            act.wait_ge(s_w[3], 48)
            act.activation(w2_hi[:], w2_raw[:], ACT.Copy).then_inc(s_whi, 1)
            layernorm(0, 0)
            edges_high(0, 0)
            sums_out(0, 0)
            sums_out(0, 1)
            transposed_high(0)
            layernorm(1, 1)
            edges_high(1, 1)
            for t in range(2):
                hidden_high(t)
                transposed_high(t + 1)
                layernorm(t + 2, t % 2)
                edges_high(t + 2, t % 2)
            with act.Fori(1, TILES // 2 - 1) as i:
                for h in range(2):
                    hidden_high(2 * i + h)
                    transposed_high(2 * i + (h + 1))
                    layernorm(2 * i + (h + 2), h)
                    edges_high(2 * i + (h + 2), h)
            hidden_high(TILES - 2)
            transposed_high(TILES - 1)
            hidden_high(TILES - 1, later=False)

        @block.vector
        def _(dve):
            dve.wait_ge(s_dst, 48)
            dve.tensor_copy(lasts[:], dst_a[:].rearrange("p (g r) -> p g r", r=GR)[:, :, GR - 1]).then_inc(s_srch, 1)
            dve.tensor_tensor(falls[:], dst_a[:], dst_b[:], ALU.is_gt).then_inc(s_srch, 1)
            dve.wait_ge(s_srch, 2)
            dve.tensor_reduce(fall[:], falls[:], AX_X, ALU.max).then_inc(s_fall, 1)
            dve.wait_ge(s_const, 1)
            for g in range(GP):
                dve.tensor_scalar(below[:, g, :], thresholds[:].rearrange("p k t -> p (k t)"), lasts[:, g:g + 1],
                                  None, ALU.is_gt).then_inc(s_below, 1)
            found = PS[:].rearrange("p a b -> p (a b)")
            dve.wait_ge(s_found, 1)
            dve.tensor_scalar(start_f[:], found[0:1, 0:KS * TILES], float(GR), float(CAP), ALU.mult,
                              ALU.min).then_inc(s_srch, 1)
            dve.tensor_scalar(end_f[:], found[0:1, TILES:KS * TILES], float(GR), float(E - GR), ALU.mult,
                              ALU.min).then_inc(s_srch, 1)
            dve.wait_ge(s_srch, 4)
            dve.tensor_copy(start_i[:], start_f[:]).then_inc(s_srch, 1)
            dve.tensor_tensor(reach[:], end_f[:], start_f[:, 0:SUB * TILES], ALU.subtract).then_inc(s_srch, 1)
            dve.wait_ge(s_srch, 6)
            dve.tensor_reduce(longest[:], reach[:], AX_X, ALU.max).then_inc(s_srch, 1)
            dve.wait_ge(s_srch, 7)
            dve.tensor_scalar(misfit[:], longest[:], float(P - GR), None, ALU.is_gt).then_inc(s_srch, 1)
            dve.wait_ge(s_srch, 8)
            dve.tensor_tensor(flag_f[:], PA[0:1, 0:1], misfit[:], ALU.add).then_inc(s_srch, 1)
            dve.wait_ge(s_srch, 9)
            dve.tensor_copy(flag_i[:], flag_f[:]).then_inc(s_start, 1)

            dve.wait_ge(s_whi, 5)
            dve.tensor_tensor(w1_lo[:], w1_raw[:], w1_hi[:], ALU.subtract).then_inc(s_wlo, 1)
            dve.tensor_tensor(wb_lo[0:DE, :], wa_raw[0:DE, :], wa_hi[0:DE, :], ALU.subtract).then_inc(s_wlo, 1)
            dve.tensor_tensor(wb_lo[96:P, :], b1_raw[96:P, :], b1_hi[96:P, :], ALU.subtract).then_inc(s_wlo, 1)
            dve.tensor_tensor(w2_lo[:], w2_raw[:], w2_hi[:], ALU.subtract).then_inc(s_wlo, 1)

            dve.wait_ge(s_start, 1)
            flag = dve.value_load(flag_i[0:1, 0:1], min_val=0, max_val=1 << 20)
            with dve.If(flag != 0):
                dve.wait_ge(s_const, 9)
                dve.tensor_copy(start_i[:], thresholds[0:1].rearrange("p k t -> p (k t)")).then_inc(s_gst, 1)
                with dve.Fori(0, SLOTS) as i:
                    dve.wait_ge(s_gin, 32 * i + 32)
                    dve.tensor_copy(g_dstf[:], g_dst[:]).then_inc(s_gv, 1)
                    dve.wait_ge(s_gv, 9 * i + 1)
                    dve.tensor_scalar(g_row[:], iota_row[0:EP, 0:EP], 0.0, g_dstf[:], ALU.mult, ALU.add).then_inc(s_gv, 1)
                    dve.wait_ge(s_gp, 2 * i + 1)
                    dve.tensor_scalar(g_same[:], PA[0:EP, 0:EP], g_dstf[:], None, ALU.is_equal).then_inc(s_gv, 1)
                    dve.tensor_scalar(g_earlier[:], iota_row[0:EP, 0:EP], part_id[0:EP, :], None, ALU.is_lt).then_inc(s_gv, 1)
                    dve.wait_ge(s_gv, 9 * i + 4)
                    dve.tensor_tensor(g_earlier[:], g_earlier[:], g_same[:], ALU.mult).then_inc(s_gv, 1)
                    dve.wait_ge(s_gv, 9 * i + 5)
                    dve.tensor_reduce(g_count[:], g_earlier[:], AX_X, ALU.max).then_inc(s_gv, 1)
                    dve.scalar_tensor_tensor(out=g_move[:], in0=part_id[0:EP, :], scalar=float(N), in1=g_dstf[:],
                                             op0=ALU.add, op1=ALU.subtract).then_inc(s_gv, 1)
                    dve.wait_ge(s_gv, 9 * i + 7)
                    dve.scalar_tensor_tensor(out=g_idx[:], in0=g_move[:], scalar=g_count[:], in1=g_dstf[:],
                                             op0=ALU.mult, op1=ALU.add).then_inc(s_gv, 1)
                    dve.wait_ge(s_gold, 16 * i + 16)
                    dve.wait_ge(s_gp, 2 * i + 2)
                    dve.tensor_tensor(g_new[:], g_old[:], PS[0:EP, 0, 0:DE + 1], ALU.add).then_inc(s_gv, 1)
                with dve.Fori(0, BLOCKS) as i:
                    dve.wait_ge(s_gn, 16 * i + 16)
                    dve.tensor_scalar(g_cnt[:], g_blk[:, :, DE:DE + 1], 1.0, None, ALU.max).then_inc(s_gnv, 1)
                    dve.wait_ge(s_gnv, 3 * i + 1)
                    dve.reciprocal(g_rcp[:], g_cnt[:]).then_inc(s_gnv, 1)
                    dve.wait_ge(s_gnv, 3 * i + 2)
                    dve.tensor_tensor(g_mean[:], g_blk[:, :, 0:DE], g_rcp[:].to_broadcast([EP, NQ, DE]),
                                      ALU.mult).then_inc(s_gnv, 1)

            def stat(t, b, js):
                if js[0] == 0:
                    dve.wait_ge(s_x[b], 16 * (t // 2 + 1) if isinstance(t, int) else 8 * t + (16 - 8 * b))
                    past(dve, s_mv, SUB * (t - 1))
                for j in js:
                    dve.bn_stats(stats[b][:, j, :], X[b][:, j, :]).then_inc(s_stats, 1)

            def aggregate(t, b):
                past(dve, s_norm, t - 1)
                dve.wait_ge(s_stats, SUB * t + SUB)
                ends(t, b)
                for j in range(SUB):
                    dve.bn_aggr(mv[b][:, j, :], stats[b][:, j, :]).then_inc(s_mv, 1)

            def ends(t, b):
                dve.wait_ge(s_win[b], 128 * (t // 2 + 1) if isinstance(t, int) else 64 * t + (128 - 64 * b))
                first = base[:, t, :] if isinstance(t, int) else base[:, bass.ds(t, 1), :].rearrange("p o j -> p (o j)")
                dve.tensor_tensor(rel[b][:], DW[b][:], first, ALU.subtract).then_inc(s_rel, 1)

            def onehot(t, b):
                dve.wait_ge(s_rel, t + 1)
                past(dve, s_sum, 2 * (t - 1))
                for j in range(SUB):
                    dve.tensor_scalar(OH[b][:, j, :], iota_row[:], rel[b][:, j:j + 1], None,
                                      ALU.is_equal).then_inc(s_oh, 1)

            def counts(t):
                dve.wait_ge(s_sc, 2 * t + 2)
                past(dve, s_agg, t)
                dve.tensor_scalar(cnt[:], SS[:, :, 2 * DE], 1.0, None, ALU.max).then_inc(s_cnt, 1)
                dve.wait_ge(s_cnt, t + 1)
                dve.reciprocal(rcp[:], cnt[:]).then_inc(s_rcp, 1)

            def transposed_low(t):
                for c in range(CD):
                    dve.wait_ge(s_hhi, 2 * t + c + 1)
                    dve.tensor_tensor(HT_lo[:, c, :], PH[c][:], HT_hi[:, c, :], ALU.subtract).then_inc(s_hlo, 1)
                dve.wait_ge(s_qhi, 2 * t + 1)
                dve.tensor_tensor(QA[DE:P, :], PA[DE:P, :], QA[DE:P, :], ALU.subtract).then_inc(s_qlo, 1)

            def hidden_low(t, m):
                dve.wait_ge(s_1hi, CH * t + m + 1)
                dve.scalar_tensor_tensor(out=H1_lo[:, m, :], in0=P1[m % 2][:], scalar=0.0, in1=H1_hi[:, m, :],
                                         op0=ALU.max, op1=ALU.subtract).then_inc(s_1lo, 1)

            def residual(t, b, q):
                dve.wait_ge(s_l2, 2 * t + q + 1)
                if q == 0:
                    dve.wait_ge(s_xb, t + 1)
                    past(dve, s_out[b], 16 * (t // 2) if isinstance(t, int) else 8 * t - 8 * b)
                dve.tensor_tensor(O[b][:, 2 * q:2 * q + 2, :], P2[q][:], XB[b][:, 2 * q:2 * q + 2, :],
                                  ALU.add).then_inc(s_fin, 1)

            def prepare(t, b):
                stat(t, b, range(SUB))
                aggregate(t, b)
                onehot(t, b)

            def step(t, b, later=True, latest=True):
                hidden_low(t, 0)
                if latest:
                    stat(t + 2, b, (0, 1))
                hidden_low(t, 1)
                if latest:
                    stat(t + 2, b, (2, 3))
                if later:
                    counts(t + 1)
                hidden_low(t, 2)
                if latest:
                    aggregate(t + 2, b)
                hidden_low(t, 3)
                if later:
                    transposed_low(t + 1)
                if latest:
                    onehot(t + 2, b)
                residual(t, b, 0)
                residual(t, b, 1)

            dve.wait_ge(s_const, 9)
            prepare(0, 0)
            counts(0)
            transposed_low(0)
            prepare(1, 1)
            step(0, 0)
            step(1, 1)
            with dve.Fori(1, TILES // 2 - 1) as i:
                for h in range(2):
                    step(2 * i + h, h)
            step(TILES - 2, 0, latest=False)
            step(TILES - 1, 1, later=False, latest=False)

        @block.tensor
        def _(pe):
            found = PS[:].rearrange("p a b -> p (a b)")
            pe.wait_ge(s_const, 3)
            for g in range(GP):
                pe.wait_ge(s_below, g + 1)
                last = pe.matmul(found[0:1, 0:KS * TILES], ones_bf[0:EP, :], below[:, g, :], start=(g == 0),
                                 stop=(g == GP - 1))
                if g == 0:
                    pe.wait_ge(s_fall, 1)
                    pe.matmul(PA[0:1, 0:1], ones_f[0:EP, :], fall[:], start=True, stop=True)
            last.then_inc(s_found, 1)

            pe.wait_ge(s_const, 14)
            pe.wait_ge(s_start, 1)
            flag = pe.value_load(flag_i[0:1, 0:1], min_val=0, max_val=1 << 20)
            with pe.If(flag != 0):
                with pe.Fori(0, SLOTS) as i:
                    pe.wait_ge(s_gv, 9 * i + 2)
                    pe.transpose(PA[0:EP, 0:EP], g_row[:], ident[0:EP, 0:EP]).then_inc(s_gp, 1)
                    pe.wait_ge(s_gv, 9 * i + 3)
                    pe.matmul(PS[0:EP, 0, 0:DE + 1], g_same[:], g_edges[:], start=True, stop=True).then_inc(s_gp, 1)

            def edge_sums(t, b, q):
                if q == 0:
                    pe.wait_ge(s_oh, SUB * t + SUB)
                    pe.wait_ge(s_elo, t + 1)
                past(pe, s_sc, 2 * t + q)
                for j in range(2):
                    k = 2 * q + j
                    last = pe.matmul(PS[:, j, 0:2 * DE + 2], OH[b][:, k, :], ES[b][:, k, :], start=True, stop=True)
                last.then_inc(s_sum, 1)

            def transposes(t, b):
                pe.wait_ge(s_ln, SUB * t + SUB)
                past(pe, s_hlo, 2 * t)
                for c in range(CD):
                    for j in range(SUB):
                        last = pe.transpose(PH[c][:, j * P:(j + 1) * P], HN[b][:, j, c * P:(c + 1) * P], ident[:])
                    last.then_inc(s_th, 1)
                pe.wait_ge(s_agg, t + 1)
                past(pe, s_qhi, 2 * t)
                past(pe, s_qlo, t)
                for j in range(SUB):
                    last = pe.transpose(PA[:, j * P:(j + 1) * P], AG[:, j, :, :].rearrange("p a d -> p (a d)"), ident[:])
                last.then_inc(s_ta, 1)

            def layer1(t, m):
                if m == 0:
                    pe.wait_ge(s_hlo, 2 * t + 2)
                    pe.wait_ge(s_qlo, t + 1)
                    pe.wait_ge(s_qhi, 2 * t + 2)
                past(pe, s_1lo, CH * t + m - 1)
                cols = slice(m * P, (m + 1) * P)
                terms = []
                for c in range(CD):
                    terms += [(w1_hi[:, c, cols], HT_hi[:, c, :]), (w1_hi[:, c, cols], HT_lo[:, c, :]),
                              (w1_lo[:, c, cols], HT_hi[:, c, :])]
                terms += [(wa_hi[:, cols], QA[:]), (wb_lo[:, cols], QB[:])]
                for n, (w, a) in enumerate(terms):
                    last = pe.matmul(P1[m % 2][:], w, a, start=(n == 0), stop=(n == len(terms) - 1))
                last.then_inc(s_l1, 1)

            def layer2(t):
                for j in range(SUB):
                    q = j // 2
                    if j % 2 == 0:
                        past(pe, s_fin, 2 * t + q - 1)
                    rows = slice(j * P, (j + 1) * P)
                    for m in range(CH):
                        if j == 0:
                            pe.wait_ge(s_1lo, CH * t + m + 1)
                        for n, (a, w) in enumerate(((H1_hi, w2_hi), (H1_hi, w2_lo), (H1_lo, w2_hi))):
                            last = pe.matmul(P2[q][:, j % 2, :], a[:, m, rows], w[:, m, :],
                                             start=(m == 0 and n == 0), stop=(m == CH - 1 and n == 2))
                    if j % 2 == 1:
                        last.then_inc(s_l2, 1)

            def step(t, b, later=True):
                layer1(t, 0)
                if later:
                    edge_sums(t + 1, 1 - b, 0)
                layer1(t, 1)
                if later:
                    edge_sums(t + 1, 1 - b, 1)
                layer1(t, 2)
                layer1(t, 3)
                if later:
                    transposes(t + 1, 1 - b)
                layer2(t)

            edge_sums(0, 0, 0)
            edge_sums(0, 0, 1)
            transposes(0, 0)
            pe.wait_ge(s_wlo, 4)
            step(0, 0)
            step(1, 1)
            with pe.Fori(1, TILES // 2 - 1) as i:
                for h in range(2):
                    step(2 * i + h, h)
            step(TILES - 2, 0)
            step(TILES - 1, 1, later=False)


_INS = ["x", "src", "dst", "edge_attr_64", "L0_gnn_W1", "L0_gnn_b1", "L0_gnn_W2", "L0_gnn_b2"]


def kernel(**inputs):
    import numpy as _np
    import concourse.bacc as _bacc
    from concourse import mybir as _mybir
    from concourse.bass_utils import run_bass_kernel_spmd as _run

    nc = _bacc.Bacc("TRN2", target_bir_lowering=False, num_devices=1)
    arrays, args = {}, []
    for name in _INS:
        a = _np.ascontiguousarray(inputs[name])
        arrays[f"in_{name}_dram"] = a
        args.append(nc.dram_tensor(f"in_{name}_dram", a.shape, _mybir.dt.from_np(a.dtype), kind="ExternalInput").ap())
    shape = arrays["in_x_dram"].shape
    args.append(nc.dram_tensor("out_0_dram", shape, _mybir.dt.float32, kind="ExternalOutput").ap())
    build(nc, *args)
    r = _run(nc, [arrays], core_ids=[0])
    return r.results[0]["out_0_dram"]
```

```python
from contextlib import ExitStack

import concourse.bass as bass
from concourse import mybir

ALU = mybir.AluOpType
ACT = mybir.ActivationFunctionType
AX_X = mybir.AxisListType.X
F32 = mybir.dt.float32
F32R = mybir.dt.float32r
BF16 = mybir.dt.bfloat16
I32 = mybir.dt.int32
U32 = mybir.dt.uint32

P = 128
SUB = 4
TILE = SUB * P
EPS = 1e-5


def past(eng, sem, value):
    if not isinstance(value, int) or value > 0:
        eng.wait_ge(sem, value)


def build(nc, x, src, dst, edge_attr, w1, b1, w2, b2, out):
    N, D = x.shape
    E, DE = edge_attr.shape
    H = w1.shape[1]
    CD, CH = D // P, H // P
    assert w1.shape[0] == DE + D and w2.shape == (H, D) and 2 * DE == P and CD == 2 and CH == 4

    TILES = -(-N // TILE)
    LAST = N - TILE
    NEW = (TILES - 1) * TILE - LAST
    assert TILES % 2 == 0 and N % TILE

    EP, GR = 125, 10
    ER_ = E // EP
    GP = ER_ // GR
    assert EP * GP * GR == E
    KS = SUB + 1
    CAP = E - P

    SLOTS = E // EP
    NQ = 16
    BLOCKS = N // (EP * NQ)
    assert BLOCKS * EP * NQ == N

    with ExitStack() as ctx:
        def sb(name, shape, dt=F32):
            return ctx.enter_context(nc.sbuf_tensor(name, shape, dt))

        def ps(name, shape, dt=F32):
            return ctx.enter_context(nc.psum_tensor(name, shape, dt))

        def sem(name):
            return ctx.enter_context(nc.semaphore(name))

        ident = sb("ident", [P, P])
        iota_row = sb("iota_row", [P, P])
        part_id = sb("part_id", [P, 1])
        base = sb("base", [P, TILES, SUB])
        half = sb("half", [P, SUB])
        eps = sb("eps", [P, SUB])
        ones_bf = sb("ones_bf", [P, 1], BF16)
        ones_f = sb("ones_f", [P, 1])
        b2_row = sb("b2_row", [P, D])
        w1_raw = sb("w1_raw", [P, CD, H])
        wa_raw = sb("wa_raw", [P, H])
        b1_raw = sb("b1_raw", [P, H])
        w2_raw = sb("w2_raw", [P, CH, D])
        w1_hi = sb("w1_hi", [P, CD, H], F32R)
        w1_lo = sb("w1_lo", [P, CD, H], F32R)
        wa_hi = sb("wa_hi", [P, H], F32R)
        wb_lo = sb("wb_lo", [P, H], F32R)
        b1_hi = sb("b1_hi", [P, H], F32R)
        w2_both = sb("w2_both", [P, CH, 2, D], F32R)

        dst_a = sb("dst_a", [EP, ER_], I32)
        dst_b = sb("dst_b", [EP, ER_], I32)
        lasts = sb("lasts", [EP, GP])
        thresholds = sb("thresholds", [EP, KS, TILES])
        below = sb("below", [EP, GP, KS * TILES], BF16)
        falls = sb("falls", [EP, ER_])
        fall = sb("fall", [EP, 1])
        start_f = sb("start_f", [1, KS * TILES])
        start_i = sb("start_i", [1, KS * TILES], I32)
        end_f = sb("end_f", [1, SUB * TILES])
        reach = sb("reach", [1, SUB * TILES])
        longest = sb("longest", [1, 1])
        misfit = sb("misfit", [1, 1])
        flag_f = sb("flag_f", [1, 1])
        flag_i = sb("flag_i", [1, 1], I32)

        X = [sb(f"X{b}", [P, SUB, D]) for b in range(2)]
        XB = [sb(f"XB{b}", [P, SUB, D]) for b in range(2)]
        O = [sb(f"O{b}", [P, SUB, D]) for b in range(2)]
        HN = [sb(f"HN{b}", [P, SUB, D]) for b in range(2)]
        stats = [sb(f"stats{b}", [P, SUB, 6]) for b in range(2)]
        mv = [sb(f"mv{b}", [P, SUB, 2]) for b in range(2)]
        veps = [sb(f"veps{b}", [P, SUB]) for b in range(2)]
        negm = [sb(f"negm{b}", [P, SUB]) for b in range(2)]
        rstd = [sb(f"rstd{b}", [P, SUB]) for b in range(2)]
        shift = [sb(f"shift{b}", [P, SUB]) for b in range(2)]
        ER = [sb(f"ER{b}", [P, SUB, DE]) for b in range(2)]
        DW = [sb(f"DW{b}", [P, SUB], I32) for b in range(2)]
        rel = [sb(f"rel{b}", [P, SUB]) for b in range(2)]
        ES = [sb(f"ES{b}", [P, SUB, 2 * DE + 2], F32R) for b in range(2)]
        OH = [sb(f"OH{b}", [P, SUB, P], F32R) for b in range(2)]
        cnt = sb("cnt", [P, SUB])
        rcp = sb("rcp", [P, SUB])
        SS = sb("SS", [P, SUB, 2 * DE + 2])
        sums = sb("sums", [P, SUB, DE])
        AG = sb("AG", [P, SUB, DE])
        HT_hi = sb("HT_hi", [P, CD, TILE], F32R)
        HT_lo = sb("HT_lo", [P, CD, TILE], F32R)
        QA = sb("QA", [P, TILE], F32R)
        QB = sb("QB", [P, TILE], F32R)
        H1_hi = sb("H1_hi", [P, CH, TILE], F32R)
        H1_lo = sb("H1_lo", [P, CH, TILE], F32R)

        g_dst = sb("g_dst", [EP, 1], I32)
        g_dstf = sb("g_dstf", [EP, 1])
        g_row = sb("g_row", [EP, EP])
        g_same = sb("g_same", [EP, EP])
        g_earlier = sb("g_earlier", [EP, EP])
        g_count = sb("g_count", [EP, 1])
        g_move = sb("g_move", [EP, 1])
        g_idx = sb("g_idx", [EP, 1], I32)
        g_edges = sb("g_edges", [EP, DE + 1])
        g_old = sb("g_old", [EP, DE + 1])
        g_new = sb("g_new", [EP, DE + 1])
        g_blk = sb("g_blk", [EP, NQ, DE + 1])
        g_cnt = sb("g_cnt", [EP, NQ, 1])
        g_rcp = sb("g_rcp", [EP, NQ, 1])
        g_mean = sb("g_mean", [EP, NQ, DE])
        g_ids = sb("g_ids", [EP, N // EP], I32)
        g_sums_dram = nc.dram_tensor("g_sums_dram", (N + EP, DE + 1), F32).ap()
        g_means_dram = nc.dram_tensor("g_means_dram", (N, DE), F32).ap()
        g_ids_dram = nc.dram_tensor("g_ids_dram", (N, 1), I32).ap()

        PH = [ps(f"PH{c}", [P, TILE]) for c in range(CD)]
        PA = ps("PA", [P, TILE])
        PS = ps("PS", [P, 2, 256])
        P1 = [ps(f"P1{i}", [P, TILE]) for i in range(2)]
        P2 = [ps(f"P2{i}", [P, 2 * D]) for i in range(2)]

        def bank(t, m):
            return (P1 + P2)[m] if isinstance(t, int) and t == 0 else P1[m % 2]

        def out_bank(j):
            return (P2 + P1)[j]

        def pairs(a):
            return PA[a * DE:(a + 1) * DE, 0:2 * P].rearrange("f (q n) -> f q n", q=2)

        def halves(to, p, a):
            return to[p:p + DE, :].rearrange("f (q a n) -> f q a n", q=2, a=2)[:, :, a, :]

        s_const = sem("s_const")
        s_w = [sem(f"s_w{i}") for i in range(4)]
        s_b2 = sem("s_b2")
        s_zero = sem("s_zero")
        s_dst = sem("s_dst")
        s_dstb = sem("s_dstb")
        s_whi = sem("s_whi")
        s_wlo = sem("s_wlo")
        s_wblo = sem("s_wblo")
        s_below = sem("s_below")
        s_fall = sem("s_fall")
        s_found = sem("s_found")
        s_srch = sem("s_srch")
        s_start = sem("s_start")
        s_x = [sem(f"s_x{b}") for b in range(2)]
        s_win = [sem(f"s_win{b}") for b in range(2)]
        s_xb = sem("s_xb")
        s_stats = sem("s_stats")
        s_mv = sem("s_mv")
        s_pool = sem("s_pool")
        s_norm = sem("s_norm")
        s_ln = sem("s_ln")
        s_rel = sem("s_rel")
        s_ehi = sem("s_ehi")
        s_elo = sem("s_elo")
        s_oh = sem("s_oh")
        s_sum = sem("s_sum")
        s_sc = sem("s_sc")
        s_cnt = sem("s_cnt")
        s_rcp = sem("s_rcp")
        s_hl = sem("s_hl")
        s_agg = sem("s_agg")
        s_th = sem("s_th")
        s_ta = sem("s_ta")
        s_hhi = sem("s_hhi")
        s_hlo = sem("s_hlo")
        s_qhi = sem("s_qhi")
        s_qlo = sem("s_qlo")
        s_l1 = sem("s_l1")
        s_1hi = sem("s_1hi")
        s_1lo = sem("s_1lo")
        s_l2 = sem("s_l2")
        s_half = sem("s_half")
        s_fin = sem("s_fin")
        s_out = [sem(f"s_out{b}") for b in range(2)]
        s_gz = sem("s_gz")
        s_gstep = sem("s_gstep")
        s_gclear = sem("s_gclear")
        s_gnum = sem("s_gnum")
        s_gin = sem("s_gin")
        s_gold = sem("s_gold")
        s_gv = sem("s_gv")
        s_gp = sem("s_gp")
        s_gput = sem("s_gput")
        s_gn = sem("s_gn")
        s_gnv = sem("s_gnv")
        s_gout = sem("s_gout")
        s_gid = sem("s_gid")
        s_gst = sem("s_gst")

        block = ctx.enter_context(nc.Block())

        @block.sync
        def _(sp):
            sp.dma_start(dst_a[:], dst.rearrange("(p r) -> p r", p=EP)).then_inc(s_dst, 16)

            def load_x(t, b):
                past(sp, s_ln, SUB * (t - 1))
                past(sp, s_xb, t - 1)
                past(sp, s_elo, t - 1)
                past(sp, s_rel, t - 1)
                first = LAST if isinstance(t, int) and t == TILES - 1 else t * TILE
                rows = x[first:first + TILE, :] if isinstance(t, int) else x[bass.ds(first, TILE), :]
                sp.dma_start(X[b][:], rows.rearrange("(j p) d -> p j d", p=P)).then_inc(s_x[b], 16)

            flag = []

            def load_windows(t, b):
                where = [start_i[0:1, t + k * TILES:t + k * TILES + 1] if isinstance(t, int)
                         else start_i[0:1, bass.ds(t + k * TILES, 1)] for k in range(SUB)]
                with sp.If(flag[0] == 0):
                    for k in range(SUB):
                        s = sp.value_load(where[k], min_val=0, max_val=CAP)
                        sp.dma_start(ER[b][:, k, :], edge_attr[bass.ds(s, P), :]).then_inc(s_win[b], 16)
                        sp.dma_start(DW[b][:, k:k + 1],
                                     dst[bass.ds(s, P)].rearrange("(p o) -> p o", o=1)).then_inc(s_win[b], 16)
                with sp.Else():
                    for k in range(SUB):
                        s = sp.value_load(where[k], min_val=0, max_val=N - P)
                        sp.dma_start(ER[b][:, k, :], g_means_dram[bass.ds(s, P), :]).then_inc(s_win[b], 16)
                        sp.dma_start(DW[b][:, k:k + 1], g_ids_dram[bass.ds(s, P), :]).then_inc(s_win[b], 16)

            def store(t, b):
                sp.wait_ge(s_fin, SUB * t + SUB)
                if isinstance(t, int) and t == TILES - 1:
                    j, p = NEW // P, NEW % P
                    rows = out[N - TILE + NEW:N - TILE + (j + 1) * P, :]
                    sp.dma_start(rows, O[b][p:P, j, :]).then_inc(s_out[b], 16)
                    sp.dma_start(out[N - TILE + (j + 1) * P:N, :].rearrange("(j p) d -> p j d", p=P),
                                 O[b][:, j + 1:SUB, :]).then_inc(s_out[b], 16)
                else:
                    rows = out[t * TILE:(t + 1) * TILE, :] if isinstance(t, int) else out[bass.ds(t * TILE, TILE), :]
                    sp.dma_start(rows.rearrange("(j p) d -> p j d", p=P), O[b][:]).then_inc(s_out[b], 16)

            load_x(0, 0)
            sp.wait_ge(s_zero, 1)
            sp.dma_start(dst_b[0:EP - 1, :],
                         dst[1:1 + (EP - 1) * ER_].rearrange("(p r) -> p r", r=ER_)).then_inc(s_dstb, 16)
            sp.dma_start(dst_b[EP - 1:EP, 0:ER_ - 1],
                         dst[1 + (EP - 1) * ER_:E].rearrange("(p r) -> p r", p=1)).then_inc(s_dstb, 16)
            load_x(1, 1)
            sp.wait_ge(s_start, 1)
            flag.append(sp.value_load(flag_i[0:1, 0:1], min_val=0, max_val=1 << 20))
            with sp.If(flag[0] != 0):
                sp.wait_ge(s_gout, 16 * BLOCKS)
                sp.wait_ge(s_gid, 16)
                sp.wait_ge(s_gst, 1)
            load_windows(0, 0)
            load_windows(1, 1)
            load_x(2, 0)
            load_windows(2, 0)
            for t in range(2):
                load_x(t + 3, (t + 3) % 2)
                load_windows(t + 3, (t + 3) % 2)
                store(t, t % 2)
            with sp.Fori(1, TILES // 2 - 2) as i:
                for h in range(2):
                    load_x(2 * i + (h + 3), (h + 3) % 2)
                    load_windows(2 * i + (h + 3), (h + 3) % 2)
                    store(2 * i + h, h)
            for t in range(TILES - 4, TILES):
                if t + 3 < TILES:
                    load_x(t + 3, (t + 3) % 2)
                    load_windows(t + 3, (t + 3) % 2)
                store(t, t % 2)
            sp.wait_ge(s_out[0], 16 * (TILES // 2))
            sp.wait_ge(s_out[1], 16 * (TILES // 2 + 1))

        @block.gpsimd
        def _(pool):
            pool.memset(dst_b[:], 1 << 20).then_inc(s_zero, 1)
            pool.memset(b1_raw[:], 0.0).then_inc(s_zero, 1)
            pool.iota(thresholds[:], pattern=[[P, KS], [TILE, TILES]], base=0, channel_multiplier=0,
                      allow_small_or_imprecise_dtypes=True).then_inc(s_zero, 1)
            pool.wait_ge(s_zero, 3)
            pool.iota(thresholds[:, :, TILES - 1:TILES], pattern=[[P, KS], [0, 1]], base=LAST, channel_multiplier=0,
                      allow_small_or_imprecise_dtypes=True).then_inc(s_const, 1)
            pool.memset(ones_bf[:], 1.0).then_inc(s_const, 1)
            pool.memset(ones_f[:], 1.0).then_inc(s_const, 1)
            pool.iota(iota_row[:], pattern=[[1, P]], base=0, channel_multiplier=0,
                      allow_small_or_imprecise_dtypes=True).then_inc(s_const, 1)
            pool.iota(part_id[:], pattern=[[0, 1]], base=0, channel_multiplier=1,
                      allow_small_or_imprecise_dtypes=True).then_inc(s_const, 1)
            pool.memset(half[:], -0.5).then_inc(s_const, 1)
            pool.memset(eps[:], EPS).then_inc(s_const, 1)
            pool.iota(base[:], pattern=[[TILE, TILES], [P, SUB]], base=0, channel_multiplier=0,
                      allow_small_or_imprecise_dtypes=True).then_inc(s_const, 1)
            pool.wait_ge(s_const, 8)
            pool.iota(base[:, TILES - 1, :], pattern=[[P, SUB]], base=LAST, channel_multiplier=0,
                      allow_small_or_imprecise_dtypes=True).then_inc(s_const, 1)
            for b in range(2):
                pool.memset(ES[b][:, :, 2 * DE:].bitcast(F32), 1.0).then_inc(s_const, 1)
            pool.wait_ge(s_const, 11)
            pool.memset(QB[DE:P, :].bitcast(F32), 1.0).then_inc(s_const, 1)
            pool.wait_ge(s_const, 12)
            pool.memset(ident[:], 0.0).then_inc(s_const, 1)
            pool.wait_ge(s_const, 13)
            pool.affine_select(out=ident[:], in_=ident[:], compare_op=ALU.not_equal, fill=1.0, base=0,
                               pattern=[[-1, P]], channel_multiplier=1).then_inc(s_const, 1)

            def norm(t, b):
                pool.wait_ge(s_mv, SUB * t + SUB)
                past(pool, s_ln, SUB * (t - 1))
                pool.tensor_tensor(veps[b][:], mv[b][:, :, 1], eps[:], ALU.add).then_inc(s_pool, 1)
                pool.tensor_scalar(negm[b][:], mv[b][:, :, 0], -1.0, None, ALU.mult).then_inc(s_pool, 1)
                pool.wait_ge(s_pool, 3 * t + 2)
                pool.tensor_tensor(rstd[b][:], veps[b][:], half[:], ALU.pow).then_inc(s_pool, 1)
                pool.wait_ge(s_pool, 3 * t + 3)
                pool.tensor_tensor(shift[b][:], negm[b][:], rstd[b][:], ALU.mult).then_inc(s_norm, 1)

            def edges(t, b):
                pool.wait_ge(s_ehi, t + 1)
                pool.tensor_tensor(ES[b][:, :, DE:2 * DE], ER[b][:], ES[b][:, :, 0:DE],
                                   ALU.subtract).then_inc(s_elo, 1)

            def residual_in(t, b):
                past(pool, s_fin, SUB * (t - 1))
                pool.wait_ge(s_x[b], 16 * (t // 2 + 1) if isinstance(t, int) else 8 * t + (16 - 8 * b))
                pool.tensor_tensor(XB[b][:], X[b][:], b2_row[:].unsqueeze(1).to_broadcast([P, SUB, D]),
                                   ALU.add).then_inc(s_xb, 1)

            def means(t):
                pool.wait_ge(s_sc, 2 * t + 2)
                pool.tensor_tensor(sums[:], SS[:, :, 0:DE], SS[:, :, DE:2 * DE], ALU.add).then_inc(s_hl, 1)
                pool.wait_ge(s_hl, t + 1)
                pool.wait_ge(s_rcp, t + 1)
                past(pool, s_ta, t)
                pool.tensor_tensor(AG[:], sums[:], rcp[:].unsqueeze(2).to_broadcast([P, SUB, DE]),
                                   ALU.mult).then_inc(s_agg, 1)

            pool.wait_ge(s_whi, 1)
            pool.tensor_tensor(w1_lo[:], w1_raw[:], w1_hi[:], ALU.subtract).then_inc(s_wlo, 1)
            pool.wait_ge(s_whi, 5)
            pool.tensor_tensor(w2_both[:, :, 1, :], w2_raw[:], w2_both[:, :, 0, :], ALU.subtract).then_inc(s_wlo, 1)
            for t in range(2):
                norm(t, t)
                if t == 0:
                    pool.wait_ge(s_b2, 16)
                residual_in(t, t)
            pool.wait_ge(s_start, 1)
            flag = pool.value_load(flag_i[0:1, 0:1], min_val=0, max_val=1 << 20)
            with pool.If(flag != 0):
                zero = below[:, 0:GP // 2, :].rearrange("p a b -> p (a b)").bitcast(F32)
                width = zero.shape[1]
                pool.wait_ge(s_found, 1)
                pool.memset(zero, 0.0).then_inc(s_gz, 1)
                pool.wait_ge(s_gz, 1)
                flat = g_sums_dram.rearrange("n d -> (n d)")
                total = (N + EP) * (DE + 1)
                per = total // EP
                assert per * EP == total
                rows = flat.rearrange("(p r) -> p r", p=EP)
                pieces = [(a, min(a + width, per)) for a in range(0, per, width)]
                for a, z in pieces:
                    pool.dma_start(rows[:, a:z], zero[:, 0:z - a]).then_inc(s_gclear, 16)
                pool.iota(g_ids[:], pattern=[[1, N // EP]], base=0, channel_multiplier=N // EP).then_inc(s_gnum, 1)
                pool.wait_ge(s_gnum, 1)
                pool.dma_start(g_ids_dram.rearrange("(p r) o -> p (r o)", p=EP), g_ids[:]).then_inc(s_gid, 16)
                pool.memset(g_edges[:, DE:DE + 1], 1.0).then_inc(s_gz, 1)
                pool.wait_ge(s_gz, 2)
                pool.wait_ge(s_gclear, 16 * len(pieces))
                with pool.Fori(0, SLOTS) as i:
                    pool.dma_start(g_edges[:, 0:DE], edge_attr[bass.ds(i * EP, EP), :]).then_inc(s_gin, 16)
                    pool.dma_start(g_dst[:], dst[bass.ds(i * EP, EP)].rearrange("(p o) -> p o", o=1)).then_inc(s_gin, 16)
                    pool.wait_ge(s_gin, 32 * i + 32)
                    pool.sem_inc(s_gstep, 1)
                    pool.indirect_dma_start(g_old[:], None, g_sums_dram[:, :],
                                            bass.IndirectOffsetOnAxis(ap=g_dst[:].bitcast(U32), axis=0)).then_inc(s_gold, 16)
                    pool.wait_ge(s_gv, 9 * i + 9)
                    pool.sem_inc(s_gstep, 1)
                    pool.indirect_dma_start(g_sums_dram[:, :],
                                            bass.IndirectOffsetOnAxis(ap=g_idx[:].bitcast(U32), axis=0),
                                            g_new[:], None).then_inc(s_gput, 16)
                    pool.wait_ge(s_gput, 16 * i + 16)
                with pool.Fori(0, BLOCKS) as i:
                    pool.dma_start(g_blk[:], g_sums_dram[bass.ds(i * (EP * NQ), EP * NQ), :]
                                   .rearrange("(p q) d -> p q d", p=EP)).then_inc(s_gn, 16)
                    pool.wait_ge(s_gnv, 3 * i + 3)
                    pool.dma_start(g_means_dram[bass.ds(i * (EP * NQ), EP * NQ), :]
                                   .rearrange("(p q) d -> p q d", p=EP), g_mean[:]).then_inc(s_gout, 16)
                    pool.wait_ge(s_gout, 16 * i + 16)
            edges(0, 0)
            means(0)
            edges(1, 1)
            for t in range(2):
                means(t + 1)
                norm(t + 2, t % 2)
                edges(t + 2, t % 2)
                residual_in(t + 2, t % 2)
            with pool.Fori(1, TILES // 2 - 1) as i:
                for h in range(2):
                    means(2 * i + (h + 1))
                    norm(2 * i + (h + 2), h)
                    edges(2 * i + (h + 2), h)
                    residual_in(2 * i + (h + 2), h)
            means(TILES - 1)

        @block.scalar
        def _(act):
            act.dma_start(b2_row[:], b2.rearrange("(o d) -> o d", o=1).to_broadcast([P, D])).then_inc(s_b2, 16)
            act.dma_start(w1_raw[:], w1[DE:DE + D, :].rearrange("(c p) h -> p c h", p=P)).then_inc(s_w[0], 16)
            for a in range(2):
                act.dma_start(wa_raw[a * DE:(a + 1) * DE, :], w1[0:DE, :]).then_inc(s_w[1], 16)
            act.wait_ge(s_zero, 3)
            for p in (64, 96):
                act.dma_start(b1_raw[p:p + 1, :], b1.rearrange("(o h) -> o h", o=1)).then_inc(s_w[2], 16)
            for a in range(2):
                act.dma_start(w2_raw[:, 2 * a:2 * a + 2, :],
                              w2[2 * a * P:2 * (a + 1) * P, :].rearrange("(c p) d -> p c d", p=P)).then_inc(s_w[3], 16)

            def layernorm(t, b):
                past(act, s_th, 2 * (t - 1))
                act.wait_ge(s_norm, t + 1)
                for j in range(SUB):
                    act.activation(HN[b][:, j, :], X[b][:, j, :], ACT.Relu, bias=shift[b][:, j:j + 1],
                                   scale=rstd[b][:, j:j + 1]).then_inc(s_ln, 1)

            def edges_high(t, b):
                act.wait_ge(s_win[b], 128 * (t // 2 + 1) if isinstance(t, int) else 64 * t + (128 - 64 * b))
                past(act, s_sum, 2 * (t - 1))
                act.activation(ES[b][:, :, 0:DE], ER[b][:], ACT.Copy).then_inc(s_ehi, 1)

            def transposed_high(t):
                past(act, s_l1, CH * t)
                for c in range(CD):
                    act.wait_ge(s_th, 2 * t + c + 1)
                    act.activation(HT_hi[:, c, :], PH[c][:], ACT.Copy).then_inc(s_hhi, 1)

            def means_high(t):
                past(act, s_l1, CH * t)
                act.wait_ge(s_ta, t + 1)
                for a in range(2):
                    act.activation(halves(QB, 0, a), pairs(a), ACT.Copy).then_inc(s_qhi, 1)
                act.wait_ge(s_qhi, 3 * t + 2)
                act.activation(QA[0:DE, :], QB[0:DE, :], ACT.Copy).then_inc(s_qhi, 1)

            def sums_out(t, q):
                act.wait_ge(s_sum, 2 * t + q + 1)
                past(act, s_agg, t)
                act.activation(SS[:, 2 * q:2 * q + 2, :], PS[:, :, 0:2 * DE + 2], ACT.Copy).then_inc(s_sc, 1)

            def hidden_high(t, later=True):
                for m in range(CH):
                    act.wait_ge(s_l1, CH * t + m + 1)
                    if m == 0:
                        past(act, s_l2, SUB * t)
                    act.activation(H1_hi[:, m, :], bank(t, m)[:], ACT.Relu).then_inc(s_1hi, 1)
                    if m < 2 and later:
                        sums_out(t + 1, m)

            act.wait_ge(s_w[0], 16)
            act.activation(w1_hi[:], w1_raw[:], ACT.Copy).then_inc(s_whi, 1)
            act.wait_ge(s_w[1], 32)
            act.activation(wa_hi[:], wa_raw[:], ACT.Copy).then_inc(s_whi, 1)
            act.wait_ge(s_w[2], 32)
            act.activation(b1_hi[DE:P, :], b1_raw[DE:P, :], ACT.Copy).then_inc(s_whi, 1)
            act.activation(wb_lo[64:96, :], b1_raw[64:96, :], ACT.Copy).then_inc(s_whi, 1)
            act.wait_ge(s_w[3], 32)
            act.activation(w2_both[:, :, 0, :], w2_raw[:], ACT.Copy).then_inc(s_whi, 1)
            layernorm(0, 0)
            transposed_high(0)
            layernorm(1, 1)
            edges_high(0, 0)
            sums_out(0, 0)
            sums_out(0, 1)
            means_high(0)
            edges_high(1, 1)
            for t in range(2):
                hidden_high(t)
                transposed_high(t + 1)
                means_high(t + 1)
                layernorm(t + 2, t % 2)
                edges_high(t + 2, t % 2)
            with act.Fori(1, TILES // 2 - 1) as i:
                for h in range(2):
                    hidden_high(2 * i + h)
                    transposed_high(2 * i + (h + 1))
                    means_high(2 * i + (h + 1))
                    layernorm(2 * i + (h + 2), h)
                    edges_high(2 * i + (h + 2), h)
            hidden_high(TILES - 2)
            transposed_high(TILES - 1)
            means_high(TILES - 1)
            hidden_high(TILES - 1, later=False)

        @block.vector
        def _(dve):
            def stat(t, b, js):
                if js[0] == 0:
                    dve.wait_ge(s_x[b], 16 * (t // 2 + 1) if isinstance(t, int) else 8 * t + (16 - 8 * b))
                    past(dve, s_mv, SUB * (t - 1))
                for j in js:
                    dve.bn_stats(stats[b][:, j, :], X[b][:, j, :]).then_inc(s_stats, 1)

            def ends(t, b):
                dve.wait_ge(s_win[b], 128 * (t // 2 + 1) if isinstance(t, int) else 64 * t + (128 - 64 * b))
                first = base[:, t, :] if isinstance(t, int) else base[:, bass.ds(t, 1), :].rearrange("p o j -> p (o j)")
                dve.tensor_tensor(rel[b][:], DW[b][:], first, ALU.subtract).then_inc(s_rel, 1)

            def aggregate(t, b):
                past(dve, s_norm, t - 1)
                dve.wait_ge(s_stats, SUB * t + SUB)
                if not isinstance(t, int):
                    ends(t, b)
                for j in range(SUB):
                    dve.bn_aggr(mv[b][:, j, :], stats[b][:, j, :]).then_inc(s_mv, 1)

            dve.wait_ge(s_dst, 16)
            dve.tensor_copy(lasts[:], dst_a[:].rearrange("p (g r) -> p g r", r=GR)[:, :, GR - 1]).then_inc(s_srch, 1)
            dve.wait_ge(s_srch, 1)
            dve.wait_ge(s_const, 1)
            for g in range(GP):
                dve.tensor_scalar(below[:, g, :], thresholds[:].rearrange("p k t -> p (k t)"), lasts[:, g:g + 1],
                                  None, ALU.is_gt).then_inc(s_below, 1)
            dve.wait_ge(s_dstb, 32)
            dve.tensor_tensor(falls[:], dst_a[:], dst_b[:], ALU.is_gt).then_inc(s_srch, 1)
            dve.wait_ge(s_srch, 2)
            dve.tensor_reduce(fall[:], falls[:], AX_X, ALU.max).then_inc(s_fall, 1)
            stat(0, 0, range(SUB))
            aggregate(0, 0)
            found = PS[:].rearrange("p a b -> p (a b)")
            dve.wait_ge(s_found, 1)
            dve.tensor_scalar(start_f[:], found[0:1, 0:KS * TILES], float(GR), float(CAP), ALU.mult,
                              ALU.min).then_inc(s_srch, 1)
            dve.tensor_scalar(end_f[:], found[0:1, TILES:KS * TILES], float(GR), float(E - GR), ALU.mult,
                              ALU.min).then_inc(s_srch, 1)
            dve.wait_ge(s_srch, 4)
            dve.tensor_copy(start_i[:], start_f[:]).then_inc(s_srch, 1)
            dve.tensor_tensor(reach[:], end_f[:], start_f[:, 0:SUB * TILES], ALU.subtract).then_inc(s_srch, 1)
            dve.wait_ge(s_srch, 6)
            dve.tensor_reduce(longest[:], reach[:], AX_X, ALU.max).then_inc(s_srch, 1)
            dve.wait_ge(s_srch, 7)
            dve.tensor_scalar(misfit[:], longest[:], float(P - GR), None, ALU.is_gt).then_inc(s_srch, 1)
            dve.wait_ge(s_srch, 8)
            dve.tensor_tensor(flag_f[:], PA[0:1, 0:1], misfit[:], ALU.add).then_inc(s_srch, 1)
            dve.wait_ge(s_srch, 9)
            dve.tensor_copy(flag_i[:], flag_f[:]).then_inc(s_start, 1)

            def counts(t):
                dve.wait_ge(s_sc, 2 * t + 2)
                past(dve, s_agg, t)
                dve.tensor_scalar(cnt[:], SS[:, :, 2 * DE], 1.0, None, ALU.max).then_inc(s_cnt, 1)
                dve.wait_ge(s_cnt, t + 1)
                dve.reciprocal(rcp[:], cnt[:]).then_inc(s_rcp, 1)

            def transposed_low(t):
                for c in range(CD):
                    dve.wait_ge(s_hhi, 2 * t + c + 1)
                    dve.tensor_tensor(HT_lo[:, c, :], PH[c][:], HT_hi[:, c, :], ALU.subtract).then_inc(s_hlo, 1)

            def means_low(t):
                dve.wait_ge(s_qhi, 3 * t + 2)
                for a in range(2):
                    dve.tensor_tensor(halves(QA, DE, a), pairs(a), halves(QB, 0, a), ALU.subtract).then_inc(s_qlo, 1)

            def hidden_low(t, m):
                dve.wait_ge(s_1hi, CH * t + m + 1)
                dve.scalar_tensor_tensor(out=H1_lo[:, m, :], in0=bank(t, m)[:], scalar=0.0, in1=H1_hi[:, m, :],
                                         op0=ALU.max, op1=ALU.subtract).then_inc(s_1lo, 1)

            def residual(t, b, j):
                dve.wait_ge(s_l2, SUB * t + j + 1)
                if j == 0:
                    dve.wait_ge(s_xb, t + 1)
                    past(dve, s_out[b], 16 * (t // 2) if isinstance(t, int) else 8 * t - 8 * b)
                dve.tensor_tensor(XB[b][:, j, :], out_bank(j)[:, D:2 * D], XB[b][:, j, :], ALU.add).then_inc(s_half, 1)
                dve.wait_ge(s_half, SUB * t + j + 1)
                dve.tensor_tensor(O[b][:, j, :], out_bank(j)[:, 0:D], XB[b][:, j, :], ALU.add).then_inc(s_fin, 1)

            def step(t, b, later=True, latest=True):
                hidden_low(t, 0)
                if latest:
                    stat(t + 2, b, (0, 1))
                hidden_low(t, 1)
                if latest:
                    stat(t + 2, b, (2, 3))
                if later:
                    counts(t + 1)
                hidden_low(t, 2)
                if latest:
                    aggregate(t + 2, b)
                    if isinstance(t, int):
                        ends(t + 2, b)
                    onehot(t + 2, b)
                hidden_low(t, 3)
                if later:
                    transposed_low(t + 1)
                residual(t, b, 0)
                if later:
                    means_low(t + 1)
                for j in range(1, SUB):
                    residual(t, b, j)

            transposed_low(0)
            dve.wait_ge(s_whi, 3)
            dve.tensor_tensor(wb_lo[0:DE, :], wa_raw[0:DE, :], wa_hi[0:DE, :], ALU.subtract).then_inc(s_wblo, 1)
            dve.tensor_tensor(wb_lo[96:P, :], b1_raw[96:P, :], b1_hi[96:P, :], ALU.subtract).then_inc(s_wblo, 1)
            stat(1, 1, range(SUB))
            aggregate(1, 1)
            dve.wait_ge(s_start, 1)
            flag = dve.value_load(flag_i[0:1, 0:1], min_val=0, max_val=1 << 20)
            with dve.If(flag != 0):
                dve.wait_ge(s_const, 9)
                dve.tensor_copy(start_i[:], thresholds[0:1].rearrange("p k t -> p (k t)")).then_inc(s_gst, 1)
                with dve.Fori(0, SLOTS) as i:
                    dve.wait_ge(s_gin, 32 * i + 32)
                    dve.tensor_copy(g_dstf[:], g_dst[:]).then_inc(s_gv, 1)
                    dve.wait_ge(s_gv, 9 * i + 1)
                    dve.tensor_scalar(g_row[:], iota_row[0:EP, 0:EP], 0.0, g_dstf[:], ALU.mult, ALU.add).then_inc(s_gv, 1)
                    dve.wait_ge(s_gp, 2 * i + 1)
                    dve.tensor_scalar(g_same[:], PA[0:EP, 0:EP], g_dstf[:], None, ALU.is_equal).then_inc(s_gv, 1)
                    dve.tensor_scalar(g_earlier[:], iota_row[0:EP, 0:EP], part_id[0:EP, :], None, ALU.is_lt).then_inc(s_gv, 1)
                    dve.wait_ge(s_gv, 9 * i + 4)
                    dve.tensor_tensor(g_earlier[:], g_earlier[:], g_same[:], ALU.mult).then_inc(s_gv, 1)
                    dve.wait_ge(s_gv, 9 * i + 5)
                    dve.tensor_reduce(g_count[:], g_earlier[:], AX_X, ALU.max).then_inc(s_gv, 1)
                    dve.scalar_tensor_tensor(out=g_move[:], in0=part_id[0:EP, :], scalar=float(N), in1=g_dstf[:],
                                             op0=ALU.add, op1=ALU.subtract).then_inc(s_gv, 1)
                    dve.wait_ge(s_gv, 9 * i + 7)
                    dve.scalar_tensor_tensor(out=g_idx[:], in0=g_move[:], scalar=g_count[:], in1=g_dstf[:],
                                             op0=ALU.mult, op1=ALU.add).then_inc(s_gv, 1)
                    dve.wait_ge(s_gold, 16 * i + 16)
                    dve.wait_ge(s_gp, 2 * i + 2)
                    dve.tensor_tensor(g_new[:], g_old[:], PS[0:EP, 0, 0:DE + 1], ALU.add).then_inc(s_gv, 1)
                with dve.Fori(0, BLOCKS) as i:
                    dve.wait_ge(s_gn, 16 * i + 16)
                    dve.tensor_scalar(g_cnt[:], g_blk[:, :, DE:DE + 1], 1.0, None, ALU.max).then_inc(s_gnv, 1)
                    dve.wait_ge(s_gnv, 3 * i + 1)
                    dve.reciprocal(g_rcp[:], g_cnt[:]).then_inc(s_gnv, 1)
                    dve.wait_ge(s_gnv, 3 * i + 2)
                    dve.tensor_tensor(g_mean[:], g_blk[:, :, 0:DE], g_rcp[:].to_broadcast([EP, NQ, DE]),
                                      ALU.mult).then_inc(s_gnv, 1)

            def onehot(t, b):
                dve.wait_ge(s_rel, t + 1)
                past(dve, s_sum, 2 * (t - 1))
                for j in range(SUB):
                    dve.tensor_scalar(OH[b][:, j, :], iota_row[:], rel[b][:, j:j + 1], None,
                                      ALU.is_equal).then_inc(s_oh, 1)

            dve.wait_ge(s_const, 9)
            ends(0, 0)
            onehot(0, 0)
            ends(1, 1)
            onehot(1, 1)
            counts(0)
            means_low(0)
            step(0, 0)
            step(1, 1)
            with dve.Fori(1, TILES // 2 - 1) as i:
                for h in range(2):
                    step(2 * i + h, h)
            step(TILES - 2, 0, latest=False)
            step(TILES - 1, 1, later=False, latest=False)

        @block.tensor
        def _(pe):
            found = PS[:].rearrange("p a b -> p (a b)")
            pe.wait_ge(s_const, 3)
            for g in range(GP):
                pe.wait_ge(s_below, g + 1)
                pe.matmul(found[0:1, 0:KS * TILES], ones_bf[0:EP, :], below[:, g, :], start=(g == 0), stop=(g == GP - 1))
            pe.wait_ge(s_fall, 1)
            pe.matmul(PA[0:1, 0:1], ones_f[0:EP, :], fall[:], start=True, stop=True).then_inc(s_found, 1)
            pe.wait_ge(s_const, 14)

            def edge_sums(t, b, q):
                if q == 0:
                    pe.wait_ge(s_oh, SUB * t + SUB)
                    pe.wait_ge(s_elo, t + 1)
                past(pe, s_sc, 2 * t + q)
                for j in range(2):
                    k = 2 * q + j
                    last = pe.matmul(PS[:, j, 0:2 * DE + 2], OH[b][:, k, :], ES[b][:, k, :], start=True, stop=True)
                last.then_inc(s_sum, 1)

            def transposes(t, b):
                pe.wait_ge(s_ln, SUB * t + SUB)
                past(pe, s_hlo, 2 * t)
                for c in range(CD):
                    for j in range(SUB):
                        if c == CD - 1 and j == SUB - 1 and not (isinstance(t, int) and t == 0):
                            pe.wait_ge(s_agg, t + 1)
                            past(pe, s_qhi, 3 * t)
                            past(pe, s_qlo, 2 * t)
                        last = pe.transpose(PH[c][:, j * P:(j + 1) * P], HN[b][:, j, c * P:(c + 1) * P], ident[:])
                    last.then_inc(s_th, 1)

            def mean_transposes():
                for q in range(SUB // 2):
                    last = pe.transpose(PA[:, q * P:(q + 1) * P], AG[:, 2 * q:2 * q + 2, :].rearrange("p j d -> p (j d)"),
                                        ident[:])
                last.then_inc(s_ta, 1)

            def layer1_nodes(t, m):
                if m == 0:
                    pe.wait_ge(s_hlo, 2 * t + 2)
                if not (isinstance(t, int) and t == 0):
                    if m < 2:
                        pe.wait_ge(s_fin, SUB * t + m - 1)
                    else:
                        pe.wait_ge(s_1lo, CH * t + m - 1)
                cols = slice(m * P, (m + 1) * P)
                for c in range(CD):
                    pe.matmul(bank(t, m)[:], w1_hi[:, c, cols], HT_hi[:, c, :], start=(c == 0), stop=False)
                    pe.matmul(bank(t, m)[:], w1_hi[:, c, cols], HT_lo[:, c, :], start=False, stop=False)
                    pe.matmul(bank(t, m)[:], w1_lo[:, c, cols], HT_hi[:, c, :], start=False, stop=False)

            def layer1_means(t, m):
                if m == 0:
                    pe.wait_ge(s_qlo, 2 * t + 2)
                    pe.wait_ge(s_qhi, 3 * t + 3)
                cols = slice(m * P, (m + 1) * P)
                pe.matmul(bank(t, m)[:], wa_hi[:, cols], QA[:], start=False, stop=False)
                pe.matmul(bank(t, m)[:], wb_lo[:, cols], QB[:], start=False, stop=True).then_inc(s_l1, 1)

            def layer2(t):
                if isinstance(t, int) and t == 0:
                    pe.wait_ge(s_1lo, CH)
                for j in range(SUB):
                    rows = slice(j * P, (j + 1) * P)
                    for m in range(CH):
                        if j == 0:
                            pe.wait_ge(s_1lo, CH * t + m + 1)
                        pe.matmul(out_bank(j)[:], H1_hi[:, m, rows], w2_both[:, m, :, :].rearrange("p a d -> p (a d)"),
                                  start=(m == 0), stop=False)
                        last = pe.matmul(out_bank(j)[:, 0:D], H1_lo[:, m, rows], w2_both[:, m, 0, :],
                                         start=False, stop=(m == CH - 1))
                    last.then_inc(s_l2, 1)

            def step(t, b, later=True):
                for m in range(CH):
                    if not (isinstance(t, int) and t == 0):
                        layer1_nodes(t, m)
                    layer1_means(t, m)
                    if m < 2 and later:
                        edge_sums(t + 1, 1 - b, m)
                if later:
                    transposes(t + 1, 1 - b)
                    mean_transposes()
                layer2(t)

            transposes(0, 0)
            pe.wait_ge(s_wlo, 1)
            for m in range(CH):
                layer1_nodes(0, m)
            pe.wait_ge(s_start, 1)
            flag = pe.value_load(flag_i[0:1, 0:1], min_val=0, max_val=1 << 20)
            with pe.If(flag != 0):
                with pe.Fori(0, SLOTS) as i:
                    pe.wait_ge(s_gv, 9 * i + 2)
                    pe.transpose(PA[0:EP, 0:EP], g_row[:], ident[0:EP, 0:EP]).then_inc(s_gp, 1)
                    pe.wait_ge(s_gv, 9 * i + 3)
                    pe.matmul(PS[0:EP, 0, 0:DE + 1], g_same[:], g_edges[:], start=True, stop=True).then_inc(s_gp, 1)

            edge_sums(0, 0, 0)
            edge_sums(0, 0, 1)
            pe.wait_ge(s_agg, 1)
            mean_transposes()
            pe.wait_ge(s_wlo, 2)
            pe.wait_ge(s_wblo, 2)
            pe.wait_ge(s_whi, 5)
            step(0, 0)
            step(1, 1)
            with pe.Fori(1, TILES // 2 - 1) as i:
                for h in range(2):
                    step(2 * i + h, h)
            step(TILES - 2, 0)
            step(TILES - 1, 1, later=False)


_INS = ["x", "src", "dst", "edge_attr_64", "L0_gnn_W1", "L0_gnn_b1", "L0_gnn_W2", "L0_gnn_b2"]


def kernel(**inputs):
    import numpy as _np
    import concourse.bacc as _bacc
    from concourse import mybir as _mybir
    from concourse.bass_utils import run_bass_kernel_spmd as _run

    nc = _bacc.Bacc("TRN2", target_bir_lowering=False, num_devices=1)
    arrays, args = {}, []
    for name in _INS:
        a = _np.ascontiguousarray(inputs[name])
        arrays[f"in_{name}_dram"] = a
        args.append(nc.dram_tensor(f"in_{name}_dram", a.shape, _mybir.dt.from_np(a.dtype), kind="ExternalInput").ap())
    shape = arrays["in_x_dram"].shape
    args.append(nc.dram_tensor("out_0_dram", shape, _mybir.dt.float32, kind="ExternalOutput").ap())
    build(nc, *args)
    r = _run(nc, [arrays], core_ids=[0])
    return r.results[0]["out_0_dram"]
```

```python
from contextlib import ExitStack

import concourse.bass as bass
from concourse import mybir

ALU = mybir.AluOpType
ACT = mybir.ActivationFunctionType
AX_X = mybir.AxisListType.X
F32 = mybir.dt.float32
F32R = mybir.dt.float32r
BF16 = mybir.dt.bfloat16
I32 = mybir.dt.int32
U32 = mybir.dt.uint32

P = 128
SUB = 4
TILE = SUB * P
EPS = 1e-5


def past(eng, sem, value):
    if not isinstance(value, int) or value > 0:
        eng.wait_ge(sem, value)


def build(nc, x, src, dst, edge_attr, w1, b1, w2, b2, out):
    N, D = x.shape
    E, DE = edge_attr.shape
    H = w1.shape[1]
    CD, CH = D // P, H // P
    assert w1.shape[0] == DE + D and w2.shape == (H, D) and 2 * DE == P and CD == 2 and CH == 4

    QP = 32
    QN = P // QP
    QF = D // QN
    MOVED = 16 * QN
    assert QF == CD * QP

    TILES = -(-N // TILE)
    LAST = N - TILE
    NEW = (TILES - 1) * TILE - LAST
    assert TILES % 2 == 0 and N % TILE

    EP, GR = 125, 10
    ER_ = E // EP
    GP = ER_ // GR
    assert EP * GP * GR == E
    KS = SUB + 1
    CAP = E - P

    SLOTS = E // EP
    NQ = 16
    BLOCKS = N // (EP * NQ)
    assert BLOCKS * EP * NQ == N

    with ExitStack() as ctx:
        def sb(name, shape, dt=F32):
            return ctx.enter_context(nc.sbuf_tensor(name, shape, dt))

        def ps(name, shape, dt=F32):
            return ctx.enter_context(nc.psum_tensor(name, shape, dt))

        def sem(name):
            return ctx.enter_context(nc.semaphore(name))

        ident = sb("ident", [P, P])
        iota_row = sb("iota_row", [P, P])
        iota_bf = sb("iota_bf", [P, P], BF16)
        part_id = sb("part_id", [P, 1])
        base = sb("base", [P, TILES, SUB])
        half = sb("half", [P, SUB])
        eps = sb("eps", [P, SUB])
        ones_bf = sb("ones_bf", [P, 1], BF16)
        ones_f = sb("ones_f", [P, 1])
        b2_row = sb("b2_row", [P, D])
        w1_raw = sb("w1_raw", [P, CD, H])
        wa_raw = sb("wa_raw", [P, H])
        b1_raw = sb("b1_raw", [P, H])
        w2_raw = sb("w2_raw", [P, CH, D])
        w1_hi = sb("w1_hi", [P, CD, H], F32R)
        w1_lo = sb("w1_lo", [P, CD, H], F32R)
        wa_hi = sb("wa_hi", [P, H], F32R)
        wb_lo = sb("wb_lo", [P, H], F32R)
        b1_hi = sb("b1_hi", [P, H], F32R)
        w2_both = sb("w2_both", [P, CH, 2, D], F32R)

        dst_a = sb("dst_a", [EP, ER_], I32)
        dst_b = sb("dst_b", [EP, ER_], I32)
        lasts = sb("lasts", [EP, GP])
        thresholds = sb("thresholds", [EP, KS, TILES])
        below = sb("below", [EP, GP, KS * TILES], BF16)
        falls = sb("falls", [EP, ER_])
        fall = sb("fall", [EP, 1])
        start_f = sb("start_f", [1, KS * TILES])
        start_i = sb("start_i", [1, KS * TILES], I32)
        end_f = sb("end_f", [1, SUB * TILES])
        reach = sb("reach", [1, SUB * TILES])
        longest = sb("longest", [1, 1])
        misfit = sb("misfit", [1, 1])
        flag_f = sb("flag_f", [1, 1])
        flag_i = sb("flag_i", [1, 1], I32)

        X = [sb(f"X{b}", [P, SUB, D]) for b in range(2)]
        XB = [sb(f"XB{b}", [P, SUB, D]) for b in range(2)]
        O = [sb(f"O{b}", [P, SUB, D]) for b in range(2)]
        HN = [sb(f"HN{b}", [P, SUB, D]) for b in range(2)]
        HQ = [sb(f"HQ{b}", [P, SUB * QN, QF]) for b in range(2)]
        stats = [sb(f"stats{b}", [P, SUB, 6]) for b in range(2)]
        mv = [sb(f"mv{b}", [P, SUB, 2]) for b in range(2)]
        veps = [sb(f"veps{b}", [P, SUB]) for b in range(2)]
        negm = [sb(f"negm{b}", [P, SUB]) for b in range(2)]
        rstd = [sb(f"rstd{b}", [P, SUB]) for b in range(2)]
        shift = [sb(f"shift{b}", [P, SUB]) for b in range(2)]
        ER = [sb(f"ER{b}", [P, SUB, DE]) for b in range(2)]
        DW = [sb(f"DW{b}", [P, SUB], I32) for b in range(2)]
        rel = [sb(f"rel{b}", [P, SUB]) for b in range(2)]
        ES = [sb(f"ES{b}", [P, SUB, 3 * DE + 2], BF16) for b in range(2)]
        EL = [sb(f"EL{b}", [P, SUB, DE]) for b in range(2)]
        OH = [sb(f"OH{b}", [P, SUB, P], BF16) for b in range(2)]
        cnt = sb("cnt", [P, SUB])
        rcp = sb("rcp", [P, SUB])
        SS = sb("SS", [P, SUB, 3 * DE + 1])
        ml = sb("ml", [P, SUB, DE])
        sums = sb("sums", [P, SUB, DE])
        AG = sb("AG", [P, SUB, DE])
        HT = sb("HT", [P, CD, TILE])
        HT_hi = sb("HT_hi", [P, CD, TILE], F32R)
        HT_lo = sb("HT_lo", [P, CD, TILE], F32R)
        QA = sb("QA", [P, TILE], F32R)
        QB = sb("QB", [P, TILE], F32R)
        H1_hi = sb("H1_hi", [P, CH, TILE], F32R)
        H1_lo = sb("H1_lo", [P, CH, TILE], F32R)

        g_dst = sb("g_dst", [EP, 1], I32)
        g_dstf = sb("g_dstf", [EP, 1])
        g_row = sb("g_row", [EP, EP])
        g_same = sb("g_same", [EP, EP])
        g_earlier = sb("g_earlier", [EP, EP])
        g_count = sb("g_count", [EP, 1])
        g_move = sb("g_move", [EP, 1])
        g_idx = sb("g_idx", [EP, 1], I32)
        g_edges = sb("g_edges", [EP, DE + 1])
        g_old = sb("g_old", [EP, DE + 1])
        g_new = sb("g_new", [EP, DE + 1])
        g_blk = sb("g_blk", [EP, NQ, DE + 1])
        g_cnt = sb("g_cnt", [EP, NQ, 1])
        g_rcp = sb("g_rcp", [EP, NQ, 1])
        g_mean = sb("g_mean", [EP, NQ, DE])
        g_ids = sb("g_ids", [EP, N // EP], I32)
        g_sums_dram = nc.dram_tensor("g_sums_dram", (N + EP, DE + 1), F32).ap()
        g_means_dram = nc.dram_tensor("g_means_dram", (N, DE), F32).ap()
        g_ids_dram = nc.dram_tensor("g_ids_dram", (N, 1), I32).ap()

        PA = ps("PA", [P, TILE])
        PS = ps("PS", [P, 2, 256])
        P1 = [ps(f"P1{i}", [P, TILE]) for i in range(4)]
        P2 = [ps(f"P2{i}", [P, 2 * D]) for i in range(2)]

        def bank(m):
            return P1[(m + 2) % CH]

        def out_bank(j):
            return (P2 + P1)[j]

        def pairs(a):
            return PA[a * DE:(a + 1) * DE, 0:2 * P].rearrange("f (q n) -> f q n", q=2)

        def halves(to, p, a):
            return to[p:p + DE, :].rearrange("f (q a n) -> f q a n", q=2, a=2)[:, :, a, :]

        s_const = sem("s_const")
        s_w = [sem(f"s_w{i}") for i in range(4)]
        s_b2 = sem("s_b2")
        s_zero = sem("s_zero")
        s_dst = sem("s_dst")
        s_dstb = sem("s_dstb")
        s_whi = sem("s_whi")
        s_wlo = sem("s_wlo")
        s_wblo = sem("s_wblo")
        s_below = sem("s_below")
        s_fall = sem("s_fall")
        s_found = sem("s_found")
        s_srch = sem("s_srch")
        s_start = sem("s_start")
        s_x = [sem(f"s_x{b}") for b in range(2)]
        s_win = [sem(f"s_win{b}") for b in range(2)]
        s_xb = sem("s_xb")
        s_stats = sem("s_stats")
        s_mv = sem("s_mv")
        s_pool = sem("s_pool")
        s_norm = sem("s_norm")
        s_ln = sem("s_ln")
        s_rel = sem("s_rel")
        s_ehi = sem("s_ehi")
        s_el = sem("s_el")
        s_emid = sem("s_emid")
        s_elo = sem("s_elo")
        s_oh = sem("s_oh")
        s_sum = sem("s_sum")
        s_sc = sem("s_sc")
        s_cnt = sem("s_cnt")
        s_rcp = sem("s_rcp")
        s_hl = sem("s_hl")
        s_agg = sem("s_agg")
        s_hq = [sem(f"s_hq{b}") for b in range(2)]
        s_th = sem("s_th")
        s_ta = sem("s_ta")
        s_hhi = sem("s_hhi")
        s_hlo = sem("s_hlo")
        s_qhi = sem("s_qhi")
        s_qlo = sem("s_qlo")
        s_l1 = sem("s_l1")
        s_1hi = sem("s_1hi")
        s_1lo = sem("s_1lo")
        s_l2 = sem("s_l2")
        s_half = sem("s_half")
        s_fin = sem("s_fin")
        s_out = [sem(f"s_out{b}") for b in range(2)]
        s_gz = sem("s_gz")
        s_gstep = sem("s_gstep")
        s_gclear = sem("s_gclear")
        s_gnum = sem("s_gnum")
        s_gin = sem("s_gin")
        s_gold = sem("s_gold")
        s_gv = sem("s_gv")
        s_gp = sem("s_gp")
        s_gput = sem("s_gput")
        s_gn = sem("s_gn")
        s_gnv = sem("s_gnv")
        s_gout = sem("s_gout")
        s_gid = sem("s_gid")
        s_gst = sem("s_gst")

        block = ctx.enter_context(nc.Block())

        def into_quadrants(eng, b):
            for q in range(QN):
                eng.dma_start(HQ[b][q * QP:(q + 1) * QP, :, :],
                              HN[b][:, :, q * QF:(q + 1) * QF]).then_inc(s_hq[b], 16)

        @block.sync
        def _(sp):
            def load_x(t, b):
                past(sp, s_ln, SUB * (t - 1))
                past(sp, s_xb, t - 1)
                past(sp, s_elo, t - 1)
                past(sp, s_rel, t - 1)
                first = LAST if isinstance(t, int) and t == TILES - 1 else t * TILE
                rows = x[first:first + TILE, :] if isinstance(t, int) else x[bass.ds(first, TILE), :]
                sp.dma_start(X[b][:], rows.rearrange("(j p) d -> p j d", p=P)).then_inc(s_x[b], 16)

            flag = []

            def load_windows(t, b):
                where = [start_i[0:1, t + k * TILES:t + k * TILES + 1] if isinstance(t, int)
                         else start_i[0:1, bass.ds(t + k * TILES, 1)] for k in range(SUB)]
                with sp.If(flag[0] == 0):
                    for k in range(SUB):
                        s = sp.value_load(where[k], min_val=0, max_val=CAP)
                        sp.dma_start(ER[b][:, k, :], edge_attr[bass.ds(s, P), :]).then_inc(s_win[b], 16)
                        sp.dma_start(DW[b][:, k:k + 1],
                                     dst[bass.ds(s, P)].rearrange("(p o) -> p o", o=1)).then_inc(s_win[b], 16)
                with sp.Else():
                    for k in range(SUB):
                        s = sp.value_load(where[k], min_val=0, max_val=N - P)
                        sp.dma_start(ER[b][:, k, :], g_means_dram[bass.ds(s, P), :]).then_inc(s_win[b], 16)
                        sp.dma_start(DW[b][:, k:k + 1], g_ids_dram[bass.ds(s, P), :]).then_inc(s_win[b], 16)

            def move(t, b):
                sp.wait_ge(s_ln, SUB * t + SUB)
                into_quadrants(sp, b)

            def store(t, b):
                sp.wait_ge(s_fin, SUB * t + SUB)
                if isinstance(t, int) and t == TILES - 1:
                    j, p = NEW // P, NEW % P
                    rows = out[N - TILE + NEW:N - TILE + (j + 1) * P, :]
                    sp.dma_start(rows, O[b][p:P, j, :]).then_inc(s_out[b], 16)
                    sp.dma_start(out[N - TILE + (j + 1) * P:N, :].rearrange("(j p) d -> p j d", p=P),
                                 O[b][:, j + 1:SUB, :]).then_inc(s_out[b], 16)
                else:
                    rows = out[t * TILE:(t + 1) * TILE, :] if isinstance(t, int) else out[bass.ds(t * TILE, TILE), :]
                    sp.dma_start(rows.rearrange("(j p) d -> p j d", p=P), O[b][:]).then_inc(s_out[b], 16)

            sp.dma_start(dst_a[:], dst.rearrange("(p r) -> p r", p=EP)).then_inc(s_dst, 16)
            load_x(0, 0)
            sp.wait_ge(s_zero, 1)
            sp.dma_start(dst_b[0:EP - 1, :],
                         dst[1:1 + (EP - 1) * ER_].rearrange("(p r) -> p r", r=ER_)).then_inc(s_dstb, 16)
            sp.dma_start(dst_b[EP - 1:EP, 0:ER_ - 1],
                         dst[1 + (EP - 1) * ER_:E].rearrange("(p r) -> p r", p=1)).then_inc(s_dstb, 16)
            load_x(1, 1)
            sp.wait_ge(s_start, 1)
            flag.append(sp.value_load(flag_i[0:1, 0:1], min_val=0, max_val=1 << 20))
            with sp.If(flag[0] != 0):
                sp.wait_ge(s_gout, 16 * BLOCKS)
                sp.wait_ge(s_gid, 16)
                sp.wait_ge(s_gst, 1)
            load_windows(0, 0)
            load_windows(1, 1)
            move(1, 1)
            load_x(2, 0)
            load_windows(2, 0)
            for t in range(2):
                load_x(t + 3, (t + 3) % 2)
                load_windows(t + 3, (t + 3) % 2)
                move(t + 2, t % 2)
                store(t, t % 2)
            with sp.Fori(1, TILES // 2 - 2) as i:
                for h in range(2):
                    load_x(2 * i + (h + 3), (h + 3) % 2)
                    load_windows(2 * i + (h + 3), (h + 3) % 2)
                    move(2 * i + (h + 2), h)
                    store(2 * i + h, h)
            for t in range(TILES - 4, TILES):
                if t + 3 < TILES:
                    load_x(t + 3, (t + 3) % 2)
                    load_windows(t + 3, (t + 3) % 2)
                if t + 2 < TILES:
                    move(t + 2, t % 2)
                store(t, t % 2)
            sp.wait_ge(s_out[0], 16 * (TILES // 2))
            sp.wait_ge(s_out[1], 16 * (TILES // 2 + 1))

        @block.gpsimd
        def _(pool):
            pool.memset(dst_b[:], 1 << 20).then_inc(s_zero, 1)
            pool.memset(b1_raw[:], 0.0).then_inc(s_zero, 1)
            pool.iota(thresholds[:], pattern=[[P, KS], [TILE, TILES]], base=0, channel_multiplier=0,
                      allow_small_or_imprecise_dtypes=True).then_inc(s_zero, 1)
            pool.wait_ge(s_zero, 3)
            pool.iota(thresholds[:, :, TILES - 1:TILES], pattern=[[P, KS], [0, 1]], base=LAST, channel_multiplier=0,
                      allow_small_or_imprecise_dtypes=True).then_inc(s_const, 1)
            pool.memset(ones_bf[:], 1.0).then_inc(s_const, 1)
            pool.memset(ones_f[:], 1.0).then_inc(s_const, 1)
            pool.iota(iota_row[:], pattern=[[1, P]], base=0, channel_multiplier=0,
                      allow_small_or_imprecise_dtypes=True).then_inc(s_const, 1)
            pool.iota(iota_bf[:], pattern=[[1, P]], base=0, channel_multiplier=0,
                      allow_small_or_imprecise_dtypes=True).then_inc(s_const, 1)
            pool.iota(part_id[:], pattern=[[0, 1]], base=0, channel_multiplier=1,
                      allow_small_or_imprecise_dtypes=True).then_inc(s_const, 1)
            pool.memset(half[:], -0.5).then_inc(s_const, 1)
            pool.memset(eps[:], EPS).then_inc(s_const, 1)
            pool.iota(base[:], pattern=[[TILE, TILES], [P, SUB]], base=0, channel_multiplier=0,
                      allow_small_or_imprecise_dtypes=True).then_inc(s_const, 1)
            pool.wait_ge(s_const, 9)
            pool.iota(base[:, TILES - 1, :], pattern=[[P, SUB]], base=LAST, channel_multiplier=0,
                      allow_small_or_imprecise_dtypes=True).then_inc(s_const, 1)
            for b in range(2):
                pool.memset(ES[b][:, :, 3 * DE:], 1.0).then_inc(s_const, 1)
            pool.wait_ge(s_const, 12)
            pool.memset(QB[DE:P, :].bitcast(F32), 1.0).then_inc(s_const, 1)
            pool.wait_ge(s_const, 13)
            pool.memset(ident[:], 0.0).then_inc(s_const, 1)
            pool.wait_ge(s_const, 14)
            pool.affine_select(out=ident[:], in_=ident[:], compare_op=ALU.not_equal, fill=1.0, base=0,
                               pattern=[[-1, P]], channel_multiplier=1).then_inc(s_const, 1)

            def norm(t, b):
                pool.wait_ge(s_mv, SUB * t + SUB)
                past(pool, s_ln, SUB * (t - 1))
                pool.tensor_tensor(veps[b][:], mv[b][:, :, 1], eps[:], ALU.add).then_inc(s_pool, 1)
                pool.tensor_scalar(negm[b][:], mv[b][:, :, 0], -1.0, None, ALU.mult).then_inc(s_pool, 1)
                pool.wait_ge(s_pool, 3 * t + 2)
                pool.tensor_tensor(rstd[b][:], veps[b][:], half[:], ALU.pow).then_inc(s_pool, 1)
                pool.wait_ge(s_pool, 3 * t + 3)
                pool.tensor_tensor(shift[b][:], negm[b][:], rstd[b][:], ALU.mult).then_inc(s_norm, 1)

            def edges_left(t, b):
                pool.wait_ge(s_ehi, t + 1)
                pool.tensor_tensor(EL[b][:], ER[b][:], ES[b][:, :, 0:DE], ALU.subtract).then_inc(s_el, 1)

            def edges_low(t, b):
                pool.wait_ge(s_emid, t + 1)
                pool.tensor_tensor(ES[b][:, :, 2 * DE:3 * DE], EL[b][:], ES[b][:, :, DE:2 * DE],
                                   ALU.subtract).then_inc(s_elo, 1)

            def residual_in(t, b):
                past(pool, s_fin, SUB * (t - 1))
                pool.wait_ge(s_x[b], 16 * (t // 2 + 1) if isinstance(t, int) else 8 * t + (16 - 8 * b))
                pool.tensor_tensor(XB[b][:], X[b][:], b2_row[:].unsqueeze(1).to_broadcast([P, SUB, D]),
                                   ALU.add).then_inc(s_xb, 1)

            def means(t):
                pool.wait_ge(s_sc, 2 * t + 2)
                pool.tensor_tensor(ml[:], SS[:, :, DE:2 * DE], SS[:, :, 2 * DE:3 * DE], ALU.add).then_inc(s_hl, 1)
                pool.wait_ge(s_hl, 2 * t + 1)
                pool.tensor_tensor(sums[:], SS[:, :, 0:DE], ml[:], ALU.add).then_inc(s_hl, 1)
                pool.wait_ge(s_hl, 2 * t + 2)
                pool.wait_ge(s_rcp, t + 1)
                past(pool, s_ta, t)
                pool.tensor_tensor(AG[:], sums[:], rcp[:].unsqueeze(2).to_broadcast([P, SUB, DE]),
                                   ALU.mult).then_inc(s_agg, 1)

            norm(0, 0)
            pool.wait_ge(s_whi, 1)
            pool.tensor_tensor(w1_lo[:], w1_raw[:], w1_hi[:], ALU.subtract).then_inc(s_wlo, 1)
            pool.wait_ge(s_whi, 5)
            pool.tensor_tensor(w2_both[:, :, 1, :], w2_raw[:], w2_both[:, :, 0, :], ALU.subtract).then_inc(s_wlo, 1)
            norm(1, 1)
            pool.wait_ge(s_b2, 16)
            residual_in(0, 0)
            pool.wait_ge(s_start, 1)
            flag = pool.value_load(flag_i[0:1, 0:1], min_val=0, max_val=1 << 20)
            with pool.If(flag != 0):
                zero = below[:, 0:GP // 2, :].rearrange("p a b -> p (a b)").bitcast(F32)
                width = zero.shape[1]
                pool.wait_ge(s_found, 1)
                pool.memset(zero, 0.0).then_inc(s_gz, 1)
                pool.wait_ge(s_gz, 1)
                flat = g_sums_dram.rearrange("n d -> (n d)")
                total = (N + EP) * (DE + 1)
                per = total // EP
                assert per * EP == total
                rows = flat.rearrange("(p r) -> p r", p=EP)
                pieces = [(a, min(a + width, per)) for a in range(0, per, width)]
                for a, z in pieces:
                    pool.dma_start(rows[:, a:z], zero[:, 0:z - a]).then_inc(s_gclear, 16)
                pool.iota(g_ids[:], pattern=[[1, N // EP]], base=0, channel_multiplier=N // EP).then_inc(s_gnum, 1)
                pool.wait_ge(s_gnum, 1)
                pool.dma_start(g_ids_dram.rearrange("(p r) o -> p (r o)", p=EP), g_ids[:]).then_inc(s_gid, 16)
                pool.memset(g_edges[:, DE:DE + 1], 1.0).then_inc(s_gz, 1)
                pool.wait_ge(s_gz, 2)
                pool.wait_ge(s_gclear, 16 * len(pieces))
                with pool.Fori(0, SLOTS) as i:
                    pool.dma_start(g_edges[:, 0:DE], edge_attr[bass.ds(i * EP, EP), :]).then_inc(s_gin, 16)
                    pool.dma_start(g_dst[:], dst[bass.ds(i * EP, EP)].rearrange("(p o) -> p o", o=1)).then_inc(s_gin, 16)
                    pool.wait_ge(s_gin, 32 * i + 32)
                    pool.sem_inc(s_gstep, 1)
                    pool.indirect_dma_start(g_old[:], None, g_sums_dram[:, :],
                                            bass.IndirectOffsetOnAxis(ap=g_dst[:].bitcast(U32), axis=0)).then_inc(s_gold, 16)
                    pool.wait_ge(s_gv, 9 * i + 9)
                    pool.sem_inc(s_gstep, 1)
                    pool.indirect_dma_start(g_sums_dram[:, :],
                                            bass.IndirectOffsetOnAxis(ap=g_idx[:].bitcast(U32), axis=0),
                                            g_new[:], None).then_inc(s_gput, 16)
                    pool.wait_ge(s_gput, 16 * i + 16)
                with pool.Fori(0, BLOCKS) as i:
                    pool.dma_start(g_blk[:], g_sums_dram[bass.ds(i * (EP * NQ), EP * NQ), :]
                                   .rearrange("(p q) d -> p q d", p=EP)).then_inc(s_gn, 16)
                    pool.wait_ge(s_gnv, 3 * i + 3)
                    pool.dma_start(g_means_dram[bass.ds(i * (EP * NQ), EP * NQ), :]
                                   .rearrange("(p q) d -> p q d", p=EP), g_mean[:]).then_inc(s_gout, 16)
                    pool.wait_ge(s_gout, 16 * i + 16)
            edges_left(0, 0)
            edges_low(0, 0)
            means(0)
            edges_left(1, 1)
            edges_low(1, 1)
            residual_in(1, 1)
            for t in range(2):
                means(t + 1)
                norm(t + 2, t % 2)
                edges_left(t + 2, t % 2)
                edges_low(t + 2, t % 2)
                residual_in(t + 2, t % 2)
            with pool.Fori(1, TILES // 2 - 1) as i:
                for h in range(2):
                    means(2 * i + (h + 1))
                    norm(2 * i + (h + 2), h)
                    edges_left(2 * i + (h + 2), h)
                    edges_low(2 * i + (h + 2), h)
                    residual_in(2 * i + (h + 2), h)
            means(TILES - 1)

        @block.scalar
        def _(act):
            act.dma_start(b2_row[:], b2.rearrange("(o d) -> o d", o=1).to_broadcast([P, D])).then_inc(s_b2, 16)
            for q in range(QN):
                act.dma_start(w1_raw[q * QP:(q + 1) * QP, :, :],
                              w1[DE + q * QF:DE + (q + 1) * QF, :].rearrange("(c f) h -> f c h", f=QP)).then_inc(s_w[0], 16)
            for a in range(2):
                act.dma_start(wa_raw[a * DE:(a + 1) * DE, :], w1[0:DE, :]).then_inc(s_w[1], 16)
            act.wait_ge(s_zero, 3)
            for p in (64, 96):
                act.dma_start(b1_raw[p:p + 1, :], b1.rearrange("(o h) -> o h", o=1)).then_inc(s_w[2], 16)
            for a in range(2):
                act.dma_start(w2_raw[:, 2 * a:2 * a + 2, :],
                              w2[2 * a * P:2 * (a + 1) * P, :].rearrange("(c p) d -> p c d", p=P)).then_inc(s_w[3], 16)

            def layernorm(t, b, js=range(SUB)):
                past(act, s_hq[b], MOVED * (t // 2) if isinstance(t, int) else MOVED // 2 * t - MOVED // 2 * b)
                act.wait_ge(s_norm, t + 1)
                for j in js:
                    act.activation(HN[b][:, j, :], X[b][:, j, :], ACT.Relu, bias=shift[b][:, j:j + 1],
                                   scale=rstd[b][:, j:j + 1]).then_inc(s_ln, 1)

            def edges_high(t, b):
                act.wait_ge(s_win[b], 128 * (t // 2 + 1) if isinstance(t, int) else 64 * t + (128 - 64 * b))
                past(act, s_sum, 2 * (t - 1))
                act.activation(ES[b][:, :, 0:DE], ER[b][:], ACT.Copy).then_inc(s_ehi, 1)

            def edges_middle(t, b):
                act.wait_ge(s_el, t + 1)
                act.activation(ES[b][:, :, DE:2 * DE], EL[b][:], ACT.Copy).then_inc(s_emid, 1)

            def transposed_high(t):
                past(act, s_l1, CH * t)
                for c in range(CD):
                    act.wait_ge(s_th, 2 * t + c + 1)
                    act.activation(HT_hi[:, c, :], HT[:, c, :], ACT.Copy).then_inc(s_hhi, 1)

            def means_high(t):
                past(act, s_l1, CH * t)
                act.wait_ge(s_ta, t + 1)
                for a in range(2):
                    act.activation(halves(QB, 0, a), pairs(a), ACT.Copy).then_inc(s_qhi, 1)
                act.wait_ge(s_qhi, 3 * t + 2)
                act.activation(QA[0:DE, :], QB[0:DE, :], ACT.Copy).then_inc(s_qhi, 1)

            def sums_out(t, q):
                act.wait_ge(s_sum, 2 * t + q + 1)
                past(act, s_agg, t)
                act.activation(SS[:, 2 * q:2 * q + 2, :], PS[:, :, 0:3 * DE + 1], ACT.Copy).then_inc(s_sc, 1)

            def hidden_high(t, later=True):
                for m in range(CH):
                    act.wait_ge(s_l1, CH * t + m + 1)
                    if m == 0:
                        past(act, s_l2, SUB * t)
                    act.activation(H1_hi[:, m, :], bank(m)[:], ACT.Relu).then_inc(s_1hi, 1)
                    if m < 2 and later:
                        sums_out(t + 1, m)

            act.wait_ge(s_w[0], 16 * QN)
            act.activation(w1_hi[:], w1_raw[:], ACT.Copy).then_inc(s_whi, 1)
            act.wait_ge(s_w[1], 32)
            act.activation(wa_hi[:], wa_raw[:], ACT.Copy).then_inc(s_whi, 1)
            act.wait_ge(s_w[2], 32)
            act.activation(b1_hi[DE:P, :], b1_raw[DE:P, :], ACT.Copy).then_inc(s_whi, 1)
            act.activation(wb_lo[64:96, :], b1_raw[64:96, :], ACT.Copy).then_inc(s_whi, 1)
            act.wait_ge(s_w[3], 32)
            act.activation(w2_both[:, :, 0, :], w2_raw[:], ACT.Copy).then_inc(s_whi, 1)
            layernorm(0, 0)
            act.wait_ge(s_ln, SUB)
            into_quadrants(act, 0)
            layernorm(1, 1)
            transposed_high(0)
            edges_high(0, 0)
            edges_middle(0, 0)
            sums_out(0, 0)
            sums_out(0, 1)
            means_high(0)
            edges_high(1, 1)
            edges_middle(1, 1)
            for t in range(2):
                hidden_high(t)
                transposed_high(t + 1)
                means_high(t + 1)
                edges_high(t + 2, t % 2)
                layernorm(t + 2, t % 2, (0, 1))
                edges_middle(t + 2, t % 2)
                layernorm(t + 2, t % 2, (2, 3))
            with act.Fori(1, TILES // 2 - 1) as i:
                for h in range(2):
                    hidden_high(2 * i + h)
                    transposed_high(2 * i + (h + 1))
                    means_high(2 * i + (h + 1))
                    edges_high(2 * i + (h + 2), h)
                    layernorm(2 * i + (h + 2), h, (0, 1))
                    edges_middle(2 * i + (h + 2), h)
                    layernorm(2 * i + (h + 2), h, (2, 3))
            hidden_high(TILES - 2)
            transposed_high(TILES - 1)
            means_high(TILES - 1)
            hidden_high(TILES - 1, later=False)

        @block.vector
        def _(dve):
            def stat(t, b, js):
                if js[0] == 0:
                    dve.wait_ge(s_x[b], 16 * (t // 2 + 1) if isinstance(t, int) else 8 * t + (16 - 8 * b))
                    past(dve, s_mv, SUB * (t - 1))
                for j in js:
                    dve.bn_stats(stats[b][:, j, :], X[b][:, j, :]).then_inc(s_stats, 1)

            def ends(t, b):
                dve.wait_ge(s_win[b], 128 * (t // 2 + 1) if isinstance(t, int) else 64 * t + (128 - 64 * b))
                first = base[:, t, :] if isinstance(t, int) else base[:, bass.ds(t, 1), :].rearrange("p o j -> p (o j)")
                dve.tensor_tensor(rel[b][:], DW[b][:], first, ALU.subtract).then_inc(s_rel, 1)

            def aggregate(t, b):
                past(dve, s_norm, t - 1)
                dve.wait_ge(s_stats, SUB * t + SUB)
                if not isinstance(t, int):
                    ends(t, b)
                for j in range(SUB):
                    dve.bn_aggr(mv[b][:, j, :], stats[b][:, j, :]).then_inc(s_mv, 1)

            dve.wait_ge(s_dst, 16)
            dve.tensor_copy(lasts[:], dst_a[:].rearrange("p (g r) -> p g r", r=GR)[:, :, GR - 1]).then_inc(s_srch, 1)
            dve.wait_ge(s_srch, 1)
            dve.wait_ge(s_const, 1)
            for g in range(GP):
                dve.tensor_scalar(below[:, g, :], thresholds[:].rearrange("p k t -> p (k t)"), lasts[:, g:g + 1],
                                  None, ALU.is_gt).then_inc(s_below, 1)
            dve.wait_ge(s_dstb, 32)
            dve.tensor_tensor(falls[:], dst_a[:], dst_b[:], ALU.is_gt).then_inc(s_srch, 1)
            dve.wait_ge(s_srch, 2)
            dve.tensor_reduce(fall[:], falls[:], AX_X, ALU.max).then_inc(s_fall, 1)
            stat(0, 0, range(SUB))
            aggregate(0, 0)
            found = PS[:].rearrange("p a b -> p (a b)")
            dve.wait_ge(s_found, 1)
            dve.tensor_scalar(start_f[:], found[0:1, 0:KS * TILES], float(GR), float(CAP), ALU.mult,
                              ALU.min).then_inc(s_srch, 1)
            dve.tensor_scalar(end_f[:], found[0:1, TILES:KS * TILES], float(GR), float(E - GR), ALU.mult,
                              ALU.min).then_inc(s_srch, 1)
            dve.wait_ge(s_srch, 4)
            dve.tensor_copy(start_i[:], start_f[:]).then_inc(s_srch, 1)
            dve.tensor_tensor(reach[:], end_f[:], start_f[:, 0:SUB * TILES], ALU.subtract).then_inc(s_srch, 1)
            dve.wait_ge(s_srch, 6)
            dve.tensor_reduce(longest[:], reach[:], AX_X, ALU.max).then_inc(s_srch, 1)
            dve.wait_ge(s_srch, 7)
            dve.tensor_scalar(misfit[:], longest[:], float(P - GR), None, ALU.is_gt).then_inc(s_srch, 1)
            dve.wait_ge(s_srch, 8)
            dve.tensor_tensor(flag_f[:], PA[0:1, 0:1], misfit[:], ALU.add).then_inc(s_srch, 1)
            dve.wait_ge(s_srch, 9)
            dve.tensor_copy(flag_i[:], flag_f[:]).then_inc(s_start, 1)

            def counts(t):
                dve.wait_ge(s_sc, 2 * t + 2)
                past(dve, s_agg, t)
                dve.tensor_scalar(cnt[:], SS[:, :, 3 * DE], 1.0, None, ALU.max).then_inc(s_cnt, 1)
                dve.wait_ge(s_cnt, t + 1)
                dve.reciprocal(rcp[:], cnt[:]).then_inc(s_rcp, 1)

            def transpose(t, b, c):
                if c == 0:
                    past(dve, s_hlo, 2 * t)
                    dve.wait_ge(s_hq[b], MOVED * (t // 2 + 1) if isinstance(t, int)
                                else MOVED // 2 * t + (MOVED - MOVED // 2 * b))
                dve.transpose(HT[:, c, :].rearrange("p (j n k) -> p k j n", j=SUB, k=QN),
                              HQ[b][:, :, c * QP:(c + 1) * QP].rearrange("p (k j) f -> p k j f", k=QN)).then_inc(s_th, 1)

            def transposed_low(t):
                for c in range(CD):
                    dve.wait_ge(s_hhi, 2 * t + c + 1)
                    if c == 0:
                        past(dve, s_l1, CH * t)
                    dve.tensor_tensor(HT_lo[:, c, :], HT[:, c, :], HT_hi[:, c, :], ALU.subtract).then_inc(s_hlo, 1)

            def means_low(t):
                dve.wait_ge(s_qhi, 3 * t + 2)
                for a in range(2):
                    dve.tensor_tensor(halves(QA, DE, a), pairs(a), halves(QB, 0, a), ALU.subtract).then_inc(s_qlo, 1)

            def hidden_low(t, m):
                dve.wait_ge(s_1hi, CH * t + m + 1)
                dve.scalar_tensor_tensor(out=H1_lo[:, m, :], in0=bank(m)[:], scalar=0.0, in1=H1_hi[:, m, :],
                                         op0=ALU.max, op1=ALU.subtract).then_inc(s_1lo, 1)

            def residual(t, b, j):
                dve.wait_ge(s_l2, SUB * t + j + 1)
                if j == 0:
                    dve.wait_ge(s_xb, t + 1)
                    past(dve, s_out[b], 16 * (t // 2) if isinstance(t, int) else 8 * t - 8 * b)
                dve.tensor_tensor(XB[b][:, j, :], out_bank(j)[:, D:2 * D], XB[b][:, j, :], ALU.add).then_inc(s_half, 1)
                dve.wait_ge(s_half, SUB * t + j + 1)
                dve.tensor_tensor(O[b][:, j, :], out_bank(j)[:, 0:D], XB[b][:, j, :], ALU.add).then_inc(s_fin, 1)

            def step(t, b, later=True, latest=True):
                hidden_low(t, 0)
                if latest:
                    stat(t + 2, b, (0, 1))
                hidden_low(t, 1)
                if latest:
                    stat(t + 2, b, (2, 3))
                if later:
                    counts(t + 1)
                hidden_low(t, 2)
                if latest:
                    aggregate(t + 2, b)
                    if isinstance(t, int):
                        ends(t + 2, b)
                if later:
                    transpose(t + 1, 1 - b, 0)
                hidden_low(t, 3)
                if later:
                    transpose(t + 1, 1 - b, 1)
                    transposed_low(t + 1)
                if latest:
                    onehot(t + 2, b)
                residual(t, b, 0)
                if later:
                    means_low(t + 1)
                for j in range(1, SUB):
                    residual(t, b, j)

            stat(1, 1, range(SUB))
            aggregate(1, 1)
            dve.wait_ge(s_start, 1)
            flag = dve.value_load(flag_i[0:1, 0:1], min_val=0, max_val=1 << 20)
            with dve.If(flag != 0):
                dve.wait_ge(s_const, 10)
                dve.tensor_copy(start_i[:], thresholds[0:1].rearrange("p k t -> p (k t)")).then_inc(s_gst, 1)
                with dve.Fori(0, SLOTS) as i:
                    dve.wait_ge(s_gin, 32 * i + 32)
                    dve.tensor_copy(g_dstf[:], g_dst[:]).then_inc(s_gv, 1)
                    dve.wait_ge(s_gv, 9 * i + 1)
                    dve.tensor_scalar(g_row[:], iota_row[0:EP, 0:EP], 0.0, g_dstf[:], ALU.mult, ALU.add).then_inc(s_gv, 1)
                    dve.wait_ge(s_gp, 2 * i + 1)
                    dve.tensor_scalar(g_same[:], PA[0:EP, 0:EP], g_dstf[:], None, ALU.is_equal).then_inc(s_gv, 1)
                    dve.tensor_scalar(g_earlier[:], iota_row[0:EP, 0:EP], part_id[0:EP, :], None, ALU.is_lt).then_inc(s_gv, 1)
                    dve.wait_ge(s_gv, 9 * i + 4)
                    dve.tensor_tensor(g_earlier[:], g_earlier[:], g_same[:], ALU.mult).then_inc(s_gv, 1)
                    dve.wait_ge(s_gv, 9 * i + 5)
                    dve.tensor_reduce(g_count[:], g_earlier[:], AX_X, ALU.max).then_inc(s_gv, 1)
                    dve.scalar_tensor_tensor(out=g_move[:], in0=part_id[0:EP, :], scalar=float(N), in1=g_dstf[:],
                                             op0=ALU.add, op1=ALU.subtract).then_inc(s_gv, 1)
                    dve.wait_ge(s_gv, 9 * i + 7)
                    dve.scalar_tensor_tensor(out=g_idx[:], in0=g_move[:], scalar=g_count[:], in1=g_dstf[:],
                                             op0=ALU.mult, op1=ALU.add).then_inc(s_gv, 1)
                    dve.wait_ge(s_gold, 16 * i + 16)
                    dve.wait_ge(s_gp, 2 * i + 2)
                    dve.tensor_tensor(g_new[:], g_old[:], PS[0:EP, 0, 0:DE + 1], ALU.add).then_inc(s_gv, 1)
                with dve.Fori(0, BLOCKS) as i:
                    dve.wait_ge(s_gn, 16 * i + 16)
                    dve.tensor_scalar(g_cnt[:], g_blk[:, :, DE:DE + 1], 1.0, None, ALU.max).then_inc(s_gnv, 1)
                    dve.wait_ge(s_gnv, 3 * i + 1)
                    dve.reciprocal(g_rcp[:], g_cnt[:]).then_inc(s_gnv, 1)
                    dve.wait_ge(s_gnv, 3 * i + 2)
                    dve.tensor_tensor(g_mean[:], g_blk[:, :, 0:DE], g_rcp[:].to_broadcast([EP, NQ, DE]),
                                      ALU.mult).then_inc(s_gnv, 1)

            def onehot(t, b):
                dve.wait_ge(s_rel, t + 1)
                past(dve, s_sum, 2 * (t - 1))
                for j in range(SUB):
                    dve.tensor_scalar(OH[b][:, j, :], iota_bf[:], rel[b][:, j:j + 1], None,
                                      ALU.is_equal).then_inc(s_oh, 1)

            dve.wait_ge(s_const, 10)
            transpose(0, 0, 0)
            transpose(0, 0, 1)
            transposed_low(0)
            ends(0, 0)
            onehot(0, 0)
            dve.wait_ge(s_whi, 3)
            dve.tensor_tensor(wb_lo[0:DE, :], wa_raw[0:DE, :], wa_hi[0:DE, :], ALU.subtract).then_inc(s_wblo, 1)
            dve.tensor_tensor(wb_lo[96:P, :], b1_raw[96:P, :], b1_hi[96:P, :], ALU.subtract).then_inc(s_wblo, 1)
            counts(0)
            means_low(0)
            ends(1, 1)
            onehot(1, 1)
            step(0, 0)
            step(1, 1)
            with dve.Fori(1, TILES // 2 - 1) as i:
                for h in range(2):
                    step(2 * i + h, h)
            step(TILES - 2, 0, latest=False)
            step(TILES - 1, 1, later=False, latest=False)

        @block.tensor
        def _(pe):
            found = PS[:].rearrange("p a b -> p (a b)")
            pe.wait_ge(s_const, 3)
            for g in range(GP):
                pe.wait_ge(s_below, g + 1)
                pe.matmul(found[0:1, 0:KS * TILES], ones_bf[0:EP, :], below[:, g, :], start=(g == 0), stop=(g == GP - 1))
            pe.wait_ge(s_fall, 1)
            pe.matmul(PA[0:1, 0:1], ones_f[0:EP, :], fall[:], start=True, stop=True).then_inc(s_found, 1)
            pe.wait_ge(s_const, 15)

            def edge_sums(t, b, q):
                if q == 0:
                    pe.wait_ge(s_oh, SUB * t + SUB)
                    pe.wait_ge(s_elo, t + 1)
                past(pe, s_sc, 2 * t + q)
                for j in range(2):
                    k = 2 * q + j
                    last = pe.matmul(PS[:, j, 0:3 * DE + 1], OH[b][:, k, :], ES[b][:, k, 0:3 * DE + 1], start=True,
                                     stop=True)
                last.then_inc(s_sum, 1)

            def mean_transposes(t):
                pe.wait_ge(s_agg, t + 1)
                past(pe, s_qhi, 3 * t)
                past(pe, s_qlo, 2 * t)
                for q in range(SUB // 2):
                    last = pe.transpose(PA[:, q * P:(q + 1) * P], AG[:, 2 * q:2 * q + 2, :].rearrange("p j d -> p (j d)"),
                                        ident[:])
                last.then_inc(s_ta, 1)

            def layer1_nodes(t, m):
                if m == 0:
                    pe.wait_ge(s_hlo, 2 * t + 2)
                if m >= 2:
                    past(pe, s_fin, SUB * (t - 1) + m + 1)
                cols = slice(m * P, (m + 1) * P)
                for c in range(CD):
                    pe.matmul(bank(m)[:], w1_hi[:, c, cols], HT_hi[:, c, :], start=(c == 0), stop=False)
                    pe.matmul(bank(m)[:], w1_hi[:, c, cols], HT_lo[:, c, :], start=False, stop=False)
                    pe.matmul(bank(m)[:], w1_lo[:, c, cols], HT_hi[:, c, :], start=False, stop=False)

            def layer1_means(t, m):
                if m == 0:
                    pe.wait_ge(s_qlo, 2 * t + 2)
                    pe.wait_ge(s_qhi, 3 * t + 3)
                cols = slice(m * P, (m + 1) * P)
                pe.matmul(bank(m)[:], wa_hi[:, cols], QA[:], start=False, stop=False)
                pe.matmul(bank(m)[:], wb_lo[:, cols], QB[:], start=False, stop=True).then_inc(s_l1, 1)

            def layer2(t, later):
                for j, ms in ((0, (0, 1, 2)), (1, (0, 1, 2)), (0, (3,)), (1, (3,)), (2, (0, 1, 2, 3)), (3, (0, 1, 2, 3))):
                    rows = slice(j * P, (j + 1) * P)
                    for m in ms:
                        if j == 0:
                            pe.wait_ge(s_1lo, CH * t + m + 1)
                        pe.matmul(out_bank(j)[:], H1_hi[:, m, rows], w2_both[:, m, :, :].rearrange("p a d -> p (a d)"),
                                  start=(m == 0), stop=False)
                        last = pe.matmul(out_bank(j)[:, 0:D], H1_lo[:, m, rows], w2_both[:, m, 0, :],
                                         start=False, stop=(m == CH - 1))
                    if m == CH - 1:
                        last.then_inc(s_l2, 1)
                    if j == 1 and m == 2 and later:
                        mean_transposes(t + 1)

            def step(t, b, later=True):
                for m in range(CH):
                    if not (isinstance(t, int) and t == 0):
                        layer1_nodes(t, m)
                    layer1_means(t, m)
                    if m < 2 and later:
                        edge_sums(t + 1, 1 - b, m)
                layer2(t, later)

            pe.wait_ge(s_start, 1)
            flag = pe.value_load(flag_i[0:1, 0:1], min_val=0, max_val=1 << 20)
            with pe.If(flag != 0):
                with pe.Fori(0, SLOTS) as i:
                    pe.wait_ge(s_gv, 9 * i + 2)
                    pe.transpose(PA[0:EP, 0:EP], g_row[:], ident[0:EP, 0:EP]).then_inc(s_gp, 1)
                    pe.wait_ge(s_gv, 9 * i + 3)
                    pe.matmul(PS[0:EP, 0, 0:DE + 1], g_same[:], g_edges[:], start=True, stop=True).then_inc(s_gp, 1)

            pe.wait_ge(s_wlo, 1)
            layer1_nodes(0, 0)
            layer1_nodes(0, 1)
            edge_sums(0, 0, 0)
            edge_sums(0, 0, 1)
            layer1_nodes(0, 2)
            mean_transposes(0)
            layer1_nodes(0, 3)
            pe.wait_ge(s_wlo, 2)
            pe.wait_ge(s_wblo, 2)
            pe.wait_ge(s_whi, 5)
            step(0, 0)
            step(1, 1)
            with pe.Fori(1, TILES // 2 - 1) as i:
                for h in range(2):
                    step(2 * i + h, h)
            step(TILES - 2, 0)
            step(TILES - 1, 1, later=False)


_INS = ["x", "src", "dst", "edge_attr_64", "L0_gnn_W1", "L0_gnn_b1", "L0_gnn_W2", "L0_gnn_b2"]


def kernel(**inputs):
    import numpy as _np
    import concourse.bacc as _bacc
    from concourse import mybir as _mybir
    from concourse.bass_utils import run_bass_kernel_spmd as _run

    nc = _bacc.Bacc("TRN2", target_bir_lowering=False, num_devices=1)
    arrays, args = {}, []
    for name in _INS:
        a = _np.ascontiguousarray(inputs[name])
        arrays[f"in_{name}_dram"] = a
        args.append(nc.dram_tensor(f"in_{name}_dram", a.shape, _mybir.dt.from_np(a.dtype), kind="ExternalInput").ap())
    shape = arrays["in_x_dram"].shape
    args.append(nc.dram_tensor("out_0_dram", shape, _mybir.dt.float32, kind="ExternalOutput").ap())
    build(nc, *args)
    r = _run(nc, [arrays], core_ids=[0])
    return r.results[0]["out_0_dram"]
```
